# Optimizing a Trainium2 kernel written in Bass

```python
import numpy as np
import jax
import jax.numpy as jnp

def _softmax(x, axis=-1):
    return jax.nn.softmax(x, axis=axis)

def _gelu(x):
    return jax.nn.gelu(x, approximate=True)

def _silu(x):
    return jax.nn.silu(x)

def _sigmoid(x):
    return jax.nn.sigmoid(x)

def _layernorm(x, axis=-1, eps=1e-05):
    m = jnp.mean(x, axis=axis, keepdims=True)
    v = jnp.var(x, axis=axis, keepdims=True)
    return (x - m) / jnp.sqrt(v + eps)

def _scatter_add(tgt, idx, src, axis=0):
    return tgt.at[idx].add(src)

def _segment_sum(src, seg, n):
    return jax.ops.segment_sum(src, seg, n)
kernel_name = 'mk_decoder_postln_d2_seqx_r8_b2133f'

def setup_inputs(seed: int=0):
    np.random.seed(seed)
    _w = jnp.asarray

    def _rec_inputs():
        import jax
        import jax.numpy as jnp
        _rk = jax.random.key(seed)
        x = 0.0002417 + 0.9998 * jax.random.normal(jax.random.fold_in(_rk, 1), (128, 64, 128), jnp.float32)
        _lenS = 64 - jax.random.randint(jax.random.fold_in(_rk, 7), (128,), 0, max(1, 64 // 4) + 1, jnp.int32)
        _lenS2 = 64 - jax.random.randint(jax.random.fold_in(_rk, 8), (128,), 0, max(1, 64 // 4) + 1, jnp.int32)
        _ctx_1024P = jax.random.normal(jax.random.fold_in(_rk, 11), (128, 16, 128), jnp.float32)
        _ctx_1024c = jax.random.dirichlet(jax.random.fold_in(_rk, 511), 0.3 * jnp.ones((16,), jnp.float32), (128, 64))
        _ctx_1024t = jnp.einsum('bsk,bkd->bsd', _ctx_1024c, _ctx_1024P)
        _ctx_1024t = _ctx_1024t * jax.lax.rsqrt(jnp.mean(jnp.square(_ctx_1024t)) + 1e-12) * 0.953939
        ctx_1024 = 7.22013e-05 + 1.00017 * (_ctx_1024t + 0.3 * jax.random.normal(jax.random.fold_in(_rk, 611), (128, 64, 128), jnp.float32))
        _validS = jnp.arange(64)[None, :] < _lenS[:, None]
        _validS2 = jnp.arange(64)[None, :] < _lenS2[:, None]
        _causal = jnp.tril(jnp.ones((64, 64), dtype=bool))
        mask_BxS2_if0 = jnp.where(jnp.ones((128, 64), dtype=bool), 0, 1).astype(jnp.int32)
        mask_1x1xSxS2_if1 = jnp.where(jnp.ones((1, 1, 64, 64), dtype=bool), 1, 0).astype(jnp.int32)
        return (x, ctx_1024, mask_BxS2_if0, mask_1x1xSxS2_if1)
    x, ctx_1024, mask_BxS2_if0, mask_1x1xSxS2_if1 = _rec_inputs()

    def _L0_attn_setup():
        import jax, jax.numpy as jnp
        import numpy as np
        H = 16
        E = 128
        D = E // H
        M = 128
        EPS = 1e-12
        key = jax.random.key(seed)
        ks = jax.random.split(key, 12)
        s = 0.02
        B, S = (8, 128)
        return {'hidden_states': jax.random.normal(ks[0], (B, S, E), jnp.float32), 'Wq': jax.random.normal(ks[1], (E, E), jnp.float32) * s, 'bq': jnp.zeros((E,), jnp.float32), 'Wk': jax.random.normal(ks[2], (E, E), jnp.float32) * s, 'bk': jnp.zeros((E,), jnp.float32), 'Wv': jax.random.normal(ks[3], (E, E), jnp.float32) * s, 'bv': jnp.zeros((E,), jnp.float32), 'dist_emb': jax.random.normal(ks[4], (2 * M - 1, D), jnp.float32) * s, 'Wo': jax.random.normal(ks[5], (E, E), jnp.float32) * s, 'bo': jnp.zeros((E,), jnp.float32), 'ln_gamma': jnp.ones((E,), jnp.float32), 'ln_beta': jnp.zeros((E,), jnp.float32)}
    _L0_attn_all = _L0_attn_setup()
    _L0_attn_in = {k: v for k, v in _L0_attn_all.items() if k in ('Wq', 'bq', 'Wk', 'bk', 'Wv', 'bv', 'dist_emb', 'Wo', 'bo', 'ln_gamma', 'ln_beta')}
    del _L0_attn_all

    def _L0_xattn_setup():
        import jax, jax.numpy as jnp
        import numpy as np
        import math
        B, M, D, H, NK = (4, 256, 128, 16, 5)
        HD = D // H

        def _gather_pad0(x, idx):
            Bx, Hx, W, hd = x.shape
            valid = (idx >= 0) & (idx < W)
            idxc = jnp.clip(idx, 0, W - 1).reshape(Bx, Hx, -1)
            g = jnp.take_along_axis(x, idxc[..., None], axis=2)
            g = g.reshape(idx.shape + (hd,))
            return g * valid[..., None].astype(x.dtype)
        key = jax.random.key(seed)
        ks = jax.random.split(key, 9)
        w = lambda k, shape: jax.random.normal(k, shape, jnp.float32) * 0.02
        return {'k': jax.random.normal(ks[0], (B, M, D), jnp.float32), 'v': jax.random.normal(ks[1], (B, M, D), jnp.float32), 'q': jax.random.normal(ks[2], (B, M, D), jnp.float32), 'mask': jnp.zeros((B, M), jnp.int32), 'Wk': w(ks[3], (D, D)), 'bk': jnp.zeros((D,), jnp.float32), 'Wv': w(ks[4], (D, D)), 'bv': jnp.zeros((D,), jnp.float32), 'Wq': w(ks[5], (D, D)), 'bq': jnp.zeros((D,), jnp.float32), 'Woff': w(ks[6], (H * NK, D)), 'boff': jnp.zeros((H * NK,), jnp.float32), 'Wo': w(ks[7], (D, D)), 'bo': jnp.zeros((D,), jnp.float32)}
    _L0_xattn_all = _L0_xattn_setup()
    _L0_xattn_in = {k: v for k, v in _L0_xattn_all.items() if k in ('Wk', 'bk', 'Wv', 'bv', 'Wq', 'bq', 'Woff', 'boff', 'Wo', 'bo')}
    del _L0_xattn_all

    def _L0_ffn_setup():
        import jax, jax.numpy as jnp
        import numpy as np
        D_MODEL = 128
        D_FF = 512
        N_EXPERTS = 8
        D_EXPERT = D_FF // N_EXPERTS
        TOP_K = 2
        LB_WEIGHT = 0.01
        B, S = (4, 256)

        def _top_k_softmax(logits, k):
            vals, _ = jax.lax.top_k(logits, k)
            thresh = vals[..., -1:]
            masked = jnp.where(logits >= thresh, logits, -jnp.inf)
            return jax.nn.softmax(masked, axis=-1)
        key = jax.random.key(seed)
        ks = jax.random.split(key, 8)
        x = jax.random.normal(ks[0], (B, S, D_MODEL), dtype=jnp.float32)
        w1 = jax.random.normal(ks[1], (N_EXPERTS, D_MODEL, D_EXPERT), dtype=jnp.float32) * (1.0 / np.sqrt(D_MODEL))
        b1 = jnp.zeros((N_EXPERTS, D_EXPERT), dtype=jnp.float32)
        w2 = jax.random.normal(ks[2], (N_EXPERTS, D_EXPERT, D_MODEL), dtype=jnp.float32) * (1.0 / np.sqrt(D_EXPERT))
        b2 = jnp.zeros((N_EXPERTS, D_MODEL), dtype=jnp.float32)
        centroids = jax.random.normal(ks[3], (N_EXPERTS, D_MODEL), dtype=jnp.float32) * 0.02
        w_route = jax.random.normal(ks[4], (N_EXPERTS, D_MODEL), dtype=jnp.float32) * (1.0 / np.sqrt(D_MODEL))
        return {'x': x, 'w1': w1, 'b1': b1, 'w2': w2, 'b2': b2, 'centroids': centroids, 'w_route': w_route}
    _L0_ffn_all = _L0_ffn_setup()
    _L0_ffn_in = {k: v for k, v in _L0_ffn_all.items() if k in ('w1', 'b1', 'w2', 'b2', 'centroids', 'w_route')}
    del _L0_ffn_all

    def _L1_attn_setup():
        import jax, jax.numpy as jnp
        import numpy as np
        B, T = (4, 256)
        D_MODEL = 128
        N_HEADS = 8
        HEAD_DIM = 32
        KV_LRANK = 64

        def _orthogonalize_per_head(w):
            chunks = w.reshape(N_HEADS, HEAD_DIM, D_MODEL)

            def ns(m):
                A = m @ m.T
                Bm = 1.5 * jnp.eye(HEAD_DIM, dtype=m.dtype) - 0.5 * A
                return Bm @ m
            return jax.vmap(ns)(chunks).reshape(w.shape)
        key = jax.random.key(seed)
        ks = jax.random.split(key, 6)

        def lin(k, out_dim, in_dim):
            bound = 1.0 / np.sqrt(in_dim)
            return jax.random.uniform(k, (out_dim, in_dim), jnp.float32, -bound, bound)
        Wq = _orthogonalize_per_head(lin(ks[0], N_HEADS * HEAD_DIM, D_MODEL))
        return {'x': jax.random.normal(ks[1], (B, T, D_MODEL), jnp.float32), 'Wq': Wq, 'Wkv_down': lin(ks[2], KV_LRANK, D_MODEL), 'Wk_up': lin(ks[3], N_HEADS * HEAD_DIM, KV_LRANK), 'Wv_up': lin(ks[4], N_HEADS * HEAD_DIM, KV_LRANK), 'Wo': lin(ks[5], D_MODEL, N_HEADS * HEAD_DIM)}
    _L1_attn_all = _L1_attn_setup()
    _L1_attn_in = {k: v for k, v in _L1_attn_all.items() if k in ('Wq', 'Wkv_down', 'Wk_up', 'Wv_up', 'Wo')}
    del _L1_attn_all

    def _L1_xattn_setup():
        import jax, jax.numpy as jnp
        import numpy as np
        D_MODEL = 128
        NUM_HEADS = 16
        D_K = D_MODEL // NUM_HEADS
        NEG = -1000000000.0

        def _split_heads(x):
            b, s, _ = x.shape
            return x.reshape(b, s, NUM_HEADS, D_K).transpose(0, 2, 1, 3)
        key = jax.random.key(seed)
        ks = jax.random.split(key, 12)
        B, S = (4, 256)
        s = 0.02
        return {'q': jax.random.normal(ks[0], (B, S, D_MODEL), jnp.float32), 'k': jax.random.normal(ks[1], (B, S, D_MODEL), jnp.float32), 'v': jax.random.normal(ks[2], (B, S, D_MODEL), jnp.float32), 'mask': jnp.ones((1, 1, S, S), jnp.int32), 'Wq': jax.random.normal(ks[3], (D_MODEL, D_MODEL), jnp.float32) * s, 'bq': jax.random.normal(ks[4], (D_MODEL,), jnp.float32) * s, 'Wk': jax.random.normal(ks[5], (D_MODEL, D_MODEL), jnp.float32) * s, 'bk': jax.random.normal(ks[6], (D_MODEL,), jnp.float32) * s, 'Wv': jax.random.normal(ks[7], (D_MODEL, D_MODEL), jnp.float32) * s, 'bv': jax.random.normal(ks[8], (D_MODEL,), jnp.float32) * s, 'Wo': jax.random.normal(ks[9], (D_MODEL, D_MODEL), jnp.float32) * s, 'bo': jax.random.normal(ks[10], (D_MODEL,), jnp.float32) * s}
    _L1_xattn_all = _L1_xattn_setup()
    _L1_xattn_in = {k: v for k, v in _L1_xattn_all.items() if k in ('Wq', 'bq', 'Wk', 'bk', 'Wv', 'bv', 'Wo', 'bo')}
    del _L1_xattn_all

    def _L1_ffn_setup():
        import jax, jax.numpy as jnp
        import numpy as np
        B, S, D, E, K = (4, 256, 128, 8, 2)
        EPS, W_THRES, TEMP = (0.0001, 0.1, 1.0)
        key = jax.random.key(seed)
        k1, k2, k3, k4, k5 = jax.random.split(key, 5)
        x = jax.random.normal(k1, (B, S, D), dtype=jnp.float32)
        gate_W = jax.random.normal(k2, (D, E), dtype=jnp.float32) * 0.02
        gate_b = jnp.zeros((E,), dtype=jnp.float32)
        expert_W = jax.random.normal(k3, (E, D, D), dtype=jnp.float32) * 0.02
        expert_b = jnp.zeros((E, D), dtype=jnp.float32)
        return {'x': x, 'gate_W': gate_W, 'gate_b': gate_b, 'expert_W': expert_W, 'expert_b': expert_b}
    _L1_ffn_all = _L1_ffn_setup()
    _L1_ffn_in = {k: v for k, v in _L1_ffn_all.items() if k in ('gate_W', 'gate_b', 'expert_W', 'expert_b')}
    del _L1_ffn_all
    return {'x': x, 'ctx_1024': ctx_1024, 'mask_BxS2_if0': mask_BxS2_if0, 'mask_1x1xSxS2_if1': mask_1x1xSxS2_if1, 'L0_attn_Wq': _L0_attn_in['Wq'], 'L0_attn_bq': _L0_attn_in['bq'], 'L0_attn_Wk': _L0_attn_in['Wk'], 'L0_attn_bk': _L0_attn_in['bk'], 'L0_attn_Wv': _L0_attn_in['Wv'], 'L0_attn_bv': _L0_attn_in['bv'], 'L0_attn_dist_emb': _L0_attn_in['dist_emb'], 'L0_attn_Wo': _L0_attn_in['Wo'], 'L0_attn_bo': _L0_attn_in['bo'], 'L0_attn_ln_gamma': _L0_attn_in['ln_gamma'], 'L0_attn_ln_beta': _L0_attn_in['ln_beta'], 'L0_xattn_Wk': _L0_xattn_in['Wk'], 'L0_xattn_bk': _L0_xattn_in['bk'], 'L0_xattn_Wv': _L0_xattn_in['Wv'], 'L0_xattn_bv': _L0_xattn_in['bv'], 'L0_xattn_Wq': _L0_xattn_in['Wq'], 'L0_xattn_bq': _L0_xattn_in['bq'], 'L0_xattn_Woff': _L0_xattn_in['Woff'], 'L0_xattn_boff': _L0_xattn_in['boff'], 'L0_xattn_Wo': _L0_xattn_in['Wo'], 'L0_xattn_bo': _L0_xattn_in['bo'], 'L0_ffn_w1': _L0_ffn_in['w1'], 'L0_ffn_b1': _L0_ffn_in['b1'], 'L0_ffn_w2': _L0_ffn_in['w2'], 'L0_ffn_b2': _L0_ffn_in['b2'], 'L0_ffn_centroids': _L0_ffn_in['centroids'], 'L0_ffn_w_route': _L0_ffn_in['w_route'], 'L1_attn_Wq': _L1_attn_in['Wq'], 'L1_attn_Wkv_down': _L1_attn_in['Wkv_down'], 'L1_attn_Wk_up': _L1_attn_in['Wk_up'], 'L1_attn_Wv_up': _L1_attn_in['Wv_up'], 'L1_attn_Wo': _L1_attn_in['Wo'], 'L1_xattn_Wq': _L1_xattn_in['Wq'], 'L1_xattn_bq': _L1_xattn_in['bq'], 'L1_xattn_Wk': _L1_xattn_in['Wk'], 'L1_xattn_bk': _L1_xattn_in['bk'], 'L1_xattn_Wv': _L1_xattn_in['Wv'], 'L1_xattn_bv': _L1_xattn_in['bv'], 'L1_xattn_Wo': _L1_xattn_in['Wo'], 'L1_xattn_bo': _L1_xattn_in['bo'], 'L1_ffn_gate_W': _L1_ffn_in['gate_W'], 'L1_ffn_gate_b': _L1_ffn_in['gate_b'], 'L1_ffn_expert_W': _L1_ffn_in['expert_W'], 'L1_ffn_expert_b': _L1_ffn_in['expert_b']}

def reference(x, ctx_1024, mask_BxS2_if0, mask_1x1xSxS2_if1, L0_attn_Wq, L0_attn_bq, L0_attn_Wk, L0_attn_bk, L0_attn_Wv, L0_attn_bv, L0_attn_dist_emb, L0_attn_Wo, L0_attn_bo, L0_attn_ln_gamma, L0_attn_ln_beta, L0_xattn_Wk, L0_xattn_bk, L0_xattn_Wv, L0_xattn_bv, L0_xattn_Wq, L0_xattn_bq, L0_xattn_Woff, L0_xattn_boff, L0_xattn_Wo, L0_xattn_bo, L0_ffn_w1, L0_ffn_b1, L0_ffn_w2, L0_ffn_b2, L0_ffn_centroids, L0_ffn_w_route, L1_attn_Wq, L1_attn_Wkv_down, L1_attn_Wk_up, L1_attn_Wv_up, L1_attn_Wo, L1_xattn_Wq, L1_xattn_bq, L1_xattn_Wk, L1_xattn_bk, L1_xattn_Wv, L1_xattn_bv, L1_xattn_Wo, L1_xattn_bo, L1_ffn_gate_W, L1_ffn_gate_b, L1_ffn_expert_W, L1_ffn_expert_b):
    import jax
    import jax.numpy as jnp

    def _L0_attn_ref(hidden_states, Wq, bq, Wk, bk, Wv, bv, dist_emb, Wo, bo, ln_gamma, ln_beta):
        import jax, jax.numpy as jnp
        import numpy as np
        H = 16
        E = 128
        D = E // H
        M = 128
        EPS = 1e-12
        B, S, _ = hidden_states.shape

        def heads(x):
            return x.reshape(B, S, H, D).transpose(0, 2, 1, 3)
        q = heads(hidden_states @ Wq + bq)
        k = heads(hidden_states @ Wk + bk)
        v = heads(hidden_states @ Wv + bv)
        scores = jnp.einsum('bhqd,bhkd->bhqk', q, k)
        pos_l = jnp.arange(S)[:, None]
        pos_r = jnp.arange(S)[None, :]
        dist_idx = pos_l - pos_r + M - 1
        pos_emb = dist_emb[dist_idx]
        rel_q = jnp.einsum('bhld,lrd->bhlr', q, pos_emb)
        rel_k = jnp.einsum('bhrd,lrd->bhlr', k, pos_emb)
        scores = (scores + rel_q + rel_k) / jnp.sqrt(jnp.asarray(D, scores.dtype))
        probs = jax.nn.softmax(scores, axis=-1)
        ctx = jnp.einsum('bhqk,bhkd->bhqd', probs, v)
        ctx = ctx.transpose(0, 2, 1, 3).reshape(B, S, E)
        h = ctx @ Wo + bo + hidden_states
        mu = jnp.mean(h, axis=-1, keepdims=True)
        var = jnp.mean(jnp.square(h - mu), axis=-1, keepdims=True)
        out = (h - mu) * jax.lax.rsqrt(var + EPS) * ln_gamma + ln_beta
        return out

    def _L0_xattn_ref(k, v, q, mask, Wk, bk, Wv, bv, Wq, bq, Woff, boff, Wo, bo):
        import jax, jax.numpy as jnp
        import numpy as np
        import math
        B, M, D, H, NK = (4, 256, 128, 16, 5)
        HD = D // H

        def _gather_pad0(x, idx):
            Bx, Hx, W, hd = x.shape
            valid = (idx >= 0) & (idx < W)
            idxc = jnp.clip(idx, 0, W - 1).reshape(Bx, Hx, -1)
            g = jnp.take_along_axis(x, idxc[..., None], axis=2)
            g = g.reshape(idx.shape + (hd,))
            return g * valid[..., None].astype(x.dtype)
        Bq, Q, _ = q.shape
        key_len = k.shape[1]
        K = jnp.einsum('bmd,ed->bme', k, Wk) + bk
        V = jnp.einsum('bmd,ed->bme', v, Wv) + bv
        Qp = jnp.einsum('bqd,ed->bqe', q, Wq) + bq
        off = jnp.einsum('bqd,ed->bqe', Qp, Woff) + boff
        off = off.reshape(Bq, Q, H, NK).transpose(0, 2, 1, 3)
        Kh = K.reshape(Bq, key_len, H, HD).transpose(0, 2, 1, 3)
        Vh = V.reshape(Bq, key_len, H, HD).transpose(0, 2, 1, 3)
        Qh = Qp.reshape(Bq, Q, H, HD).transpose(0, 2, 1, 3)
        loc = jnp.arange(Q, dtype=jnp.float32)[:, None]
        left = -NK // 2
        ref = jnp.arange(left, NK + left, dtype=jnp.float32)
        sign_lens = (1 - mask).sum(-1).astype(jnp.float32) - 1.0
        loc_x = jnp.mod(ref + off + loc, sign_lens[:, None, None, None])
        xg = loc_x / (key_len - 1) * 2.0 - 1.0
        ix = ((xg + 1.0) * key_len - 1.0) / 2.0
        x0 = jnp.floor(ix)
        dx = ix - x0
        i0 = x0.astype(jnp.int32)
        i1 = i0 + 1
        w0 = (1.0 - dx)[..., None]
        w1 = dx[..., None]
        sk = 0.5 * (w0 * _gather_pad0(Kh, i0) + w1 * _gather_pad0(Kh, i1))
        sv = 0.5 * (w0 * _gather_pad0(Vh, i0) + w1 * _gather_pad0(Vh, i1))
        scores = jnp.einsum('bhqd,bhqkd->bhqk', Qh / math.sqrt(HD), sk)
        attn = jax.nn.softmax(scores, axis=-1)
        ctx = jnp.einsum('bhqk,bhqkd->bhqd', attn, sv)
        ctx = ctx.transpose(0, 2, 1, 3).reshape(Bq, Q, H * HD)
        return jnp.einsum('bqd,ed->bqe', ctx, Wo) + bo

    def _L0_ffn_ref(x, w1, b1, w2, b2, centroids, w_route):
        import jax, jax.numpy as jnp
        import numpy as np
        D_MODEL = 128
        D_FF = 512
        N_EXPERTS = 8
        D_EXPERT = D_FF // N_EXPERTS
        TOP_K = 2
        LB_WEIGHT = 0.01
        B, S = (4, 256)

        def _top_k_softmax(logits, k):
            vals, _ = jax.lax.top_k(logits, k)
            thresh = vals[..., -1:]
            masked = jnp.where(logits >= thresh, logits, -jnp.inf)
            return jax.nn.softmax(masked, axis=-1)
        eps = 1e-12
        x_norm = x / jnp.maximum(jnp.linalg.norm(x, axis=-1, keepdims=True), eps)
        c_norm = centroids / jnp.maximum(jnp.linalg.norm(centroids, axis=-1, keepdims=True), eps)
        cos_scores = jnp.einsum('bsd,ed->bse', x_norm, c_norm)
        route_scores = jnp.einsum('bsd,ed->bse', x, w_route)
        logits = cos_scores + route_scores
        gates = _top_k_softmax(logits, TOP_K)
        h = jax.nn.gelu(jnp.einsum('bsd,edh->bseh', x, w1) + b1, approximate=False)
        expert_out = jnp.einsum('bseh,ehd->bsed', h, w2) + b2
        out = jnp.einsum('bse,bsed->bsd', gates, expert_out)
        return out

    def _L1_attn_ref(x, Wq, Wkv_down, Wk_up, Wv_up, Wo):
        import jax, jax.numpy as jnp
        import numpy as np
        B, T = (4, 256)
        D_MODEL = 128
        N_HEADS = 8
        HEAD_DIM = 32
        KV_LRANK = 64

        def _orthogonalize_per_head(w):
            chunks = w.reshape(N_HEADS, HEAD_DIM, D_MODEL)

            def ns(m):
                A = m @ m.T
                Bm = 1.5 * jnp.eye(HEAD_DIM, dtype=m.dtype) - 0.5 * A
                return Bm @ m
            return jax.vmap(ns)(chunks).reshape(w.shape)
        b, t, _ = x.shape
        q = (x @ Wq.T).reshape(b, t, N_HEADS, HEAD_DIM)
        kv_latent = x @ Wkv_down.T
        k = (kv_latent @ Wk_up.T).reshape(b, t, N_HEADS, HEAD_DIM)
        v = (kv_latent @ Wv_up.T).reshape(b, t, N_HEADS, HEAD_DIM)
        scale = HEAD_DIM ** (-0.5)
        scores = jnp.einsum('bqhd,bkhd->bhqk', q, k) * scale
        attn = jax.nn.softmax(scores, axis=-1)
        out = jnp.einsum('bhqk,bkhd->bqhd', attn, v)
        out = out.reshape(b, t, N_HEADS * HEAD_DIM)
        return out @ Wo.T

    def _L1_xattn_ref(q, k, v, mask, Wq, bq, Wk, bk, Wv, bv, Wo, bo):
        import jax, jax.numpy as jnp
        import numpy as np
        D_MODEL = 128
        NUM_HEADS = 16
        D_K = D_MODEL // NUM_HEADS
        NEG = -1000000000.0

        def _split_heads(x):
            b, s, _ = x.shape
            return x.reshape(b, s, NUM_HEADS, D_K).transpose(0, 2, 1, 3)
        qh = _split_heads(q @ Wq.T + bq)
        kh = _split_heads(k @ Wk.T + bk)
        vh = _split_heads(v @ Wv.T + bv)
        scores = jnp.einsum('bhqd,bhkd->bhqk', qh, kh) / jnp.sqrt(jnp.float32(D_K))
        scores = jnp.where(mask == 0, jnp.float32(NEG), scores)
        attn = jax.nn.softmax(scores, axis=-1)
        out = jnp.einsum('bhqk,bhkd->bhqd', attn, vh)
        b, h, s, dk = out.shape
        out = out.transpose(0, 2, 1, 3).reshape(b, s, D_MODEL)
        return out @ Wo.T + bo

    def _L1_ffn_ref(x, gate_W, gate_b, expert_W, expert_b):
        import jax, jax.numpy as jnp
        import numpy as np
        B, S, D, E, K = (4, 256, 128, 8, 2)
        EPS, W_THRES, TEMP = (0.0001, 0.1, 1.0)
        scores = jnp.maximum((x @ gate_W + gate_b) / TEMP, EPS)
        p = jax.nn.softmax(scores, axis=-1)
        _, topk_idx = jax.lax.top_k(p, K)
        topk_mask = jax.nn.one_hot(topk_idx, E, dtype=p.dtype).sum(-2) > 0
        w = jnp.maximum(p, W_THRES)
        w_gather = jnp.take_along_axis(w, topk_idx, axis=-1)
        total = jax.lax.stop_gradient(w_gather.sum(-1, keepdims=True))
        w = w / total
        comb = jnp.where(topk_mask, w, jnp.zeros_like(w))
        y = jnp.einsum('bsd,edf->bsef', x, expert_W) + expert_b
        out = jnp.einsum('bsef,bse->bsf', y, comb) / K
        return out
    x = _layernorm(x + _L0_attn_ref(x, L0_attn_Wq, L0_attn_bq, L0_attn_Wk, L0_attn_bk, L0_attn_Wv, L0_attn_bv, L0_attn_dist_emb, L0_attn_Wo, L0_attn_bo, L0_attn_ln_gamma, L0_attn_ln_beta), axis=-1)
    x = _layernorm(x + _L0_xattn_ref(ctx_1024, ctx_1024, x, mask_BxS2_if0, L0_xattn_Wk, L0_xattn_bk, L0_xattn_Wv, L0_xattn_bv, L0_xattn_Wq, L0_xattn_bq, L0_xattn_Woff, L0_xattn_boff, L0_xattn_Wo, L0_xattn_bo), axis=-1)
    x = _layernorm(x + _L0_ffn_ref(x, L0_ffn_w1, L0_ffn_b1, L0_ffn_w2, L0_ffn_b2, L0_ffn_centroids, L0_ffn_w_route), axis=-1)
    x = _layernorm(x + _L1_attn_ref(x, L1_attn_Wq, L1_attn_Wkv_down, L1_attn_Wk_up, L1_attn_Wv_up, L1_attn_Wo), axis=-1)
    x = _layernorm(x + _L1_xattn_ref(x, ctx_1024, ctx_1024, mask_1x1xSxS2_if1, L1_xattn_Wq, L1_xattn_bq, L1_xattn_Wk, L1_xattn_bk, L1_xattn_Wv, L1_xattn_bv, L1_xattn_Wo, L1_xattn_bo), axis=-1)
    x = _layernorm(x + _L1_ffn_ref(x, L1_ffn_gate_W, L1_ffn_gate_b, L1_ffn_expert_W, L1_ffn_expert_b), axis=-1)
    return x

_drawn_inputs = setup_inputs


def setup_inputs(seed=0):
    import zlib

    import numpy as np

    out = dict(_drawn_inputs(seed))
    spreads = {'L0_attn_bq': (0.0, 0.8),
     'L0_attn_bk': (0.0, 2.0),
     'L0_attn_bv': (0.0, 0.1),
     'L0_attn_bo': (0.0, 0.1),
     'L0_attn_ln_gamma': (1.0, 0.2),
     'L0_attn_ln_beta': (0.0, 0.1),
     'L0_xattn_bk': (0.0, 2.0),
     'L0_xattn_bv': (0.0, 0.1),
     'L0_xattn_bq': (0.0, 0.8),
     'L0_xattn_boff': (0.0, 0.726),
     'L0_xattn_bo': (0.0, 0.1),
     'L0_ffn_b1': (0.0, 0.1),
     'L0_ffn_b2': (0.0, 0.1),
     'L1_ffn_gate_b': (0.0, 0.1),
     'L1_ffn_expert_b': (0.0, 0.1)}
    factors = {'L0_attn_Wq': 8.0,
     'L0_attn_Wk': 8.0,
     'L0_attn_Wv': 3.743,
     'L0_attn_dist_emb': 8.0,
     'L0_xattn_Wk': 8.0,
     'L0_xattn_Wq': 7.882,
     'L0_xattn_Woff': 8.0,
     'L1_attn_Wq': 4.588,
     'L1_attn_Wk_up': 4.548,
     'L1_xattn_Wq': 8.0,
     'L1_xattn_bq': 64.0,
     'L1_xattn_Wk': 8.0,
     'L1_xattn_bk': 64.0,
     'L1_xattn_bv': 7.793}
    for name, (base, spread) in spreads.items():
        noise = np.random.default_rng([zlib.crc32(name.encode()), seed]).standard_normal(out[name].shape)
        drawn = base * np.exp(spread * noise) if base else spread * noise
        out[name] = jnp.asarray(drawn.astype(out[name].dtype))
    for name, factor in factors.items():
        out[name] = (out[name] * factor).astype(out[name].dtype)
    return out
```

```python
from contextlib import ExitStack

import concourse.bass as bass
from concourse import mybir

F32 = mybir.dt.float32
F16 = mybir.dt.float16
BF16 = mybir.dt.bfloat16
I32 = mybir.dt.int32
ALU = mybir.AluOpType
ACT = mybir.ActivationFunctionType
AX = mybir.AxisListType.X

B, S, D = 128, 64, 128
P = 128
TILES = B * S // P
G = 2
TURNS = TILES // G
H16, D8 = 16, 8
H8, D32 = 8, 32
NK = 5
HP = H16 // 2
NS = HP * NK * 2
LAT = 64
E = 8
WIN = 2 * S - 1
R8 = float(D8) ** -0.5
R32 = float(D32) ** -0.5
NEG = -1e9 * float(D8) ** 0.5
EPS_LN = 1e-5
QT = 4
M_SLOTS = 4
UNITS = 512

SIGNALS = {}
for _l in ("a0", "a1", "a2"):
    SIGNALS.update({
        f"{_l}_xT": 1, f"{_l}_qk": 2, f"{_l}_masked": 8, f"{_l}_v": 2, f"{_l}_shifted": 1, f"{_l}_probs": 1,
        f"{_l}_probsT0": 1, f"{_l}_probsT1": 1, f"{_l}_ctx": 1, f"{_l}_ctxT": 1, f"{_l}_xb": 1, f"{_l}_added": 1,
    })
SIGNALS.update({
    "a0_cT": 1, "a1_latent": 1, "a0_x": 1, "a1_x": 1, "a2_x": 1, "g0_x": 1, "f0_x": 1, "f1_x": 1,
    "g0_xT": 1, "g0_qT": 1, "g0_qtok": 1, "g0_pos": 1, "g0_kv": 1, "g0_hi": 1, "g0_rest": 1, "g0_mid": 1,
    "g0_table": 6, "g0_dist": 1, "g0_idx": 2, "g0_idxT": 1, "g0_hat": 1, "g0_onehotA": 6, "g0_onehotV": 4, "g0_added": 1, "f0_added": 1, "a0_summed": 1, "a2_where": 1, "f1_scored": 1, "f1_mixed": 1, "g0_sampled": 8,
    "g0_shifted": 1, "g0_probs": 1, "g0_ctx": 1, "g0_ctxT": 1, "g0_xb": 1,
    "f0_xT": 1, "f0_sq": 1, "f0_rnorm": 1, "f0_logits": 1, "f0_h": 4, "f0_shifted": 1, "f0_exp": 1,
    "f0_gates": 1, "f0_gatesT": 1, "f0_gated": 1,
    "f1_xT": 1, "f1_shifted": 1, "f1_exp": 1, "f1_p": 1, "f1_rank": 1,
})
for _n in ("a0i", "a0", "g0", "f0", "a1", "a2", "f1"):
    SIGNALS.update({f"{_n}_var": 1, f"{_n}_rstd": 1})
SIGNALS["out_x"] = 1


def psum_plan():
    plan = {"M": {}, "S": {}}
    for stage in STAGES:
        for g in range(G):
            for kind, name in STAGE_USES[stage]:
                d = plan[kind]
                n = M_SLOTS if kind == "M" else 2
                before = list(d)[len(d) - n] if len(d) >= n else None
                d[(name, g)] = (len(d) % n, len(d) // n, before)
    return plan


def attention_stages(l):
    return [f"{l}_A", f"{l}_B", f"{l}_C", f"{l}_D", f"{l}_E", f"{l}_F", f"{l}_G"]


STAGES = (attention_stages("a0") + [f"g0_{n}" for n in "ABCDEFGH"] + [f"f0_{n}" for n in "ABCDE"]
          + ["a1_A", "a1_L"] + attention_stages("a1")[1:] + attention_stages("a2") + ["f1_A", "f1_B"])
STAGE_USES = {}
for _l in ("a0", "a1", "a2"):
    STAGE_USES.update({
        f"{_l}_A": [("M", f"{_l}_xT")],
        f"{_l}_B": [("M", f"{_l}_qk"), ("M", f"{_l}_v")],
        f"{_l}_C": [("S", f"{_l}_scores")],
        f"{_l}_D": [("M", f"{_l}_pT0")] + ([("M", f"{_l}_pT1")] if _l != "a1" else []),
        f"{_l}_E": [("M", f"{_l}_pv")],
        f"{_l}_F": [("M", f"{_l}_cT")],
        f"{_l}_G": [("M", f"{_l}_o")],
    })
STAGE_USES["a1_L"] = [("M", "a1_lat")]
STAGE_USES.update({
    "g0_A": [("M", "g0_xT")],
    "g0_B": [("M", "g0_q"), ("M", "g0_kv")],
    "g0_C": [("M", "g0_off")],
    "g0_D": [("M", "g0_idxT")],
    "g0_E": [("M", f"g0_eq{n}") for n in range(10)],
    "g0_F": [("M", f"g0_s{n}") for n in range(HP)],
    "g0_G": [("M", "g0_cT")],
    "g0_H": [("M", "g0_o")],
    "f0_A": [("M", "f0_xT")],
    "f0_B": [("M", "f0_lg"), ("M", "f0_h")],
    "f0_C": [("M", "f0_gT")],
    "f0_D": [("M", "f0_gb")],
    "f0_E": [("M", "f0_o")],
    "f1_A": [("M", "f1_xT")],
    "f1_B": [("M", "f1_gs"), ("S", "f1_y")],
})


READ_BY = {"a0_scores": "a0_summed", "a1_scores": "a1_shifted", "a2_scores": "a2_where", "a1_lat": "a1_latent",
           "g0_xT": "g0_xT", "g0_q": "g0_qtok", "g0_kv": "g0_kv", "g0_off": "g0_pos", "g0_idxT": "g0_idxT",
           "f0_xT": "f0_xT", "f0_lg": "f0_logits", "f0_h": "f0_h", "f0_gT": "f0_gatesT", "f0_gb": "f0_gated",
           "f1_xT": "f1_xT", "f1_gs": "f1_scored", "f1_y": "f1_mixed", "a0_xT": "a0_cT", "a1_xT": "a1_xT", "a2_xT": "a2_xT"}
for _l in ("a0", "a1", "a2"):
    READ_BY.update({f"{_l}_qk": f"{_l}_qk", f"{_l}_v": f"{_l}_v", f"{_l}_pT0": f"{_l}_probsT0", f"{_l}_pT1": f"{_l}_probsT1",
                    f"{_l}_pv": f"{_l}_ctx"})
for _l in ("a0", "g0", "f0", "a1", "a2"):
    READ_BY.update({f"{_l}_cT": f"{_l}_ctxT", f"{_l}_o": f"{_l}_added"})
ONEHOT_BY = "AVAVAAVAVA"
for _n in range(10):
    READ_BY[f"g0_eq{_n}"] = (f"g0_onehot{ONEHOT_BY[_n]}", ONEHOT_BY[:_n + 1].count(ONEHOT_BY[_n]))
for _n in range(HP):
    READ_BY[f"g0_s{_n}"] = ("g0_sampled", _n + 1)


def spread(ap, axis, n):
    u = ap.unsqueeze(axis)
    shape = list(u.shape)
    shape[axis] = n
    return u.broadcast_to(shape)


def decoder_kernel(nc, A, out):
    tok = lambda a: a.rearrange("b s d -> (b s) d").rearrange("(t p) d -> t p d", p=P)
    x_t, ctx_t, out_t = tok(A["x"]), tok(A["ctx"]), tok(out)
    rel = nc.dram_tensor("rel_scores", [B, S, H16, S], F32, kind="Internal").ap()
    rel_t = rel.rearrange("b l h r -> (b l) (h r)").rearrange("(t p) n -> t p n", p=P)

    with ExitStack() as ctx:
        def sb(name, shape, dt=F32, c=ctx):
            return c.enter_context(nc.sbuf_tensor(name, shape, dt))

        def sem(name):
            return ctx.enter_context(nc.semaphore(name))

        psS = ctx.enter_context(nc.psum_tensor("psS", [P, 2, 2 * UNITS], F32))
        psM = ctx.enter_context(nc.psum_tensor("psM", [P, M_SLOTS, UNITS], F32))

        loaded_weights = sem("loaded_weights")
        prepared = sem("prepared")
        x4_loaded = sem("x4_loaded")
        rel_stored = sem("rel_stored")
        tiles_loaded = sem("tiles_loaded")
        out_stored = sem("out_stored")
        sig = {n: sem(n) for n in SIGNALS}
        m_full = [sem(f"m_full{i}") for i in range(M_SLOTS)]
        s_full = [sem(f"s_full{i}") for i in range(2)]
        dve_step = sem("dve_step")
        pool_step = sem("pool_step")
        turn_sems = range(sig[next(iter(SIGNALS))].num, pool_step.num + 1)

        W = {}
        for name, a in A.items():
            if name in ("x", "ctx") or name.startswith("rel_") or name.startswith("bc_"):
                continue
            W[name] = sb("w_" + name, list(a.shape), a.dtype)
        for name, a in A.items():
            if name.startswith("bc_"):
                W[name] = sb("w_" + name, [P, a.shape[-1]])
        c_normT = sb("c_normT", [P, 2 * E])
        lens = sb("lens", [P, TILES])
        lens_inv = sb("lens_inv", [P, TILES])
        lens_pos = sb("lens_pos", [P, TILES])
        mask01 = sb("mask01", [P, S])
        maskneg = sb("maskneg", [P, S])
        mhalf = sb("mhalf", [P, 1])
        emb = sb("emb", [P, 2, WIN])
        n_loads = 2 + len(W) + sum(1 for n in W if n.startswith("bc_") and A[n].shape[0] == 2) + 1
        ident = W["ident"]

        with ExitStack() as c0:
            cn = sb("cn", [E, P], c=c0)
            cn2 = sb("cn2", [E, P], c=c0)
            css = sb("css", [E, 4], c=c0)
            lrow = sb("lrow", [P, 2], c=c0)
            maskf = sb("maskf", [P, S], c=c0)
            lsel = sb("lsel", [P, 2, TILES], c=c0)
            m2 = sb("m2", [P, S], I32, c=c0)
            with nc.Block() as block:
                @block.sync
                def _(sp):
                    sp.sem_inc(rel_stored, 1)
                    sp.sem_inc(out_stored, 1)
                    for name, w in W.items():
                        a = A[name]
                        if name.startswith("bc_"):
                            rows = a.shape[0]
                            for i in range(rows):
                                n = P // rows
                                sp.dma_start(w[i * n:(i + 1) * n, :],
                                             a[i:i + 1, :].broadcast_to([n, a.shape[1]])).then_inc(loaded_weights, 16)
                        else:
                            sp.dma_start(w[:], a).then_inc(loaded_weights, 16)
                    sp.dma_start(emb[:, 0, :], A["rel_fwd"]).then_inc(loaded_weights, 16)
                    sp.dma_start(emb[:, 1, :], A["rel_rev"]).then_inc(loaded_weights, 16)
                    sp.dma_start(m2[S:P, :], A["mask_ss"]).then_inc(loaded_weights, 16)

                @block.vector
                def _(dve):
                    steps = [0]

                    def link(ins):
                        steps[0] += 1
                        ins.then_inc(dve_step, 1)
                        dve.wait_ge(dve_step, steps[0])

                    dve.wait_ge(loaded_weights, 16 * n_loads)
                    link(dve.memset(mhalf[:, :], -0.5))
                    link(dve.tensor_tensor(W["bc_off"][:, :], W["bc_off"][:, :], W["bc_ref"][:, :], ALU.add))
                    link(dve.tensor_copy(m2[0:S, :], W["mask_ss"][:, :]))
                    link(dve.tensor_scalar(mask01[:, :], m2[:, :], 0.0, None, ALU.not_equal))
                    link(dve.tensor_scalar(maskneg[:, :], mask01[:, :], -1.0, -NEG, ALU.add, ALU.mult))
                    link(dve.tensor_scalar(maskf[:, :], W["mask_bs"][:, :], -1.0, 1.0, ALU.mult, ALU.add))
                    link(dve.tensor_reduce(lrow[:, 0:1], maskf[:, :], AX, ALU.add))
                    link(dve.tensor_scalar(lrow[:, 1:2], lrow[:, 0:1], -1.0, None, ALU.add))
                    for p in range(2):
                        dve.tensor_scalar(lsel[:, p, :], W["seq_of_tile"][:, p * TILES:(p + 1) * TILES], lrow[:, 1:2],
                                          None, ALU.mult).then_inc(prepared, 1)
                    link(dve.tensor_tensor(cn2[:, :], W["centroids"][:, :], W["centroids"][:, :], ALU.mult))
                    dve.tensor_reduce(css[:, 0:1], cn2[:, :], AX, ALU.add).then_inc(prepared, 1)
                    dve.wait_ge(m_full[0], 1)
                    link(dve.tensor_copy(lens[:, :], psM[:, 0, 0:TILES]))
                    link(dve.reciprocal(lens_inv[:, :], lens[:, :]))
                    link(dve.tensor_scalar(lens_pos[:, :], lens[:, :], 0.0, None, ALU.max))
                    dve.wait_ge(pool_step, 1)
                    link(dve.tensor_scalar(css[:, 2:3], css[:, 1:2], 1e12, None, ALU.min))
                    dve.tensor_scalar(cn[:, :], W["centroids"][:, :], css[:, 2:3], None, ALU.mult).then_inc(prepared, 1)
                    dve.wait_ge(m_full[1], 1)
                    link(dve.tensor_copy(c_normT[:, 0:E], psM[:, 1, 0:E]))
                    link(dve.tensor_copy(c_normT[:, E:2 * E], W["w_routeT"][:, :]))

                @block.gpsimd
                def _(pool):
                    pool.wait_ge(prepared, 3)
                    pool.wait_ge(dve_step, 1)
                    pool.tensor_tensor(css[:, 1:2], css[:, 0:1], mhalf[0:E, :], ALU.pow).then_inc(pool_step, 1)

                @block.tensor
                def _(pe):
                    pe.wait_ge(prepared, 2)
                    pe.wait_ge(loaded_weights, 16 * n_loads)
                    for p in range(2):
                        mm = pe.matmul(psM[S * p:S * p + S, 0, 0:TILES], W["ones64"][:, :], lsel[:, p, :],
                                       start=True, stop=True)
                    mm.then_inc(m_full[0], 1)
                    pe.wait_ge(prepared, 4)
                    pe.transpose(psM[:, 1, 0:E], cn[:, :], ident[0:E, 0:E]).then_inc(m_full[1], 1)
            nc.all_engine_barrier(sems_to_clear=turn_sems)

        with ExitStack() as c1:
            q_all = sb("q_all", [P, B * S], c=c1)
            k_all = sb("k_all", [P, B * S], c=c1)
            with ExitStack() as c2:
                x4 = sb("x4", [P, QT, D], c=c2)
                xT4 = sb("xT4", [P, QT * P], c=c2)
                with nc.Fori(0, TILES // QT) as it:
                    with nc.Block() as block:
                        @block.sync
                        def _(sp):
                            sp.dma_start(x4[:, :, :], x_t[bass.ds(it * QT, QT)].rearrange("g p d -> p g d")).then_inc(
                                x4_loaded, 16)

                        @block.tensor
                        def _(pe):
                            pe.wait_ge(x4_loaded, it * 16 + 16)
                            for g in range(QT):
                                mm = pe.transpose(psM[:, 0, g * P:(g + 1) * P], x4[:, g, :], ident[:, :])
                            mm.then_inc(m_full[0], 1)
                            pe.wait_ge(sig["a0_xT"], 1)
                            pe.matmul(psM[:, 1, :], W["a0_wq"][:, :], xT4[:, :], start=True, stop=True).then_inc(m_full[1], 1)
                            pe.matmul(psM[:, 2, :], W["a0_wk"][:, :], xT4[:, :], start=True, stop=True).then_inc(m_full[2], 1)

                        @block.scalar
                        def _(act):
                            act.wait_ge(m_full[0], 1)
                            act.copy(xT4[:, :], psM[:, 0, :]).then_inc(sig["a0_xT"], 1)
                            act.wait_ge(m_full[1], 1)
                            act.activation(q_all[:, bass.ds(it * UNITS, UNITS)], psM[:, 1, :], ACT.Identity,
                                           bias=W["a0_bq"][:, 0:1])

                        @block.vector
                        def _(dve):
                            dve.wait_ge(m_full[2], 1)
                            dve.tensor_scalar(k_all[:, bass.ds(it * UNITS, UNITS)], psM[:, 2, :], W["a0_bk"][:, 0:1],
                                              None, ALU.add)
                    nc.all_engine_barrier(sems_to_clear=turn_sems)

            with ExitStack() as c2:
                rbuf = [sb(f"rbuf{i}", [P, S, 2, S], c=c2) for i in range(2)]
                epair = sb("epair", [P, 2, 2, 2, WIN], c=c2)
                q_l = q_all[:, :].rearrange("p (b s) -> p s b", s=S)
                k_r = k_all[:, :].rearrange("p (b s) -> p s b", s=S)
                CH = 4
                NCH = S // CH
                banks = [psM[:, i, :] for i in range(M_SLOTS)] + [psS[:, i // 2, (i % 2) * UNITS:(i % 2 + 1) * UNITS] for i in range(4)]
                k_full, q_full, k_free, q_free, pair_ready = (sig[n] for n in list(SIGNALS)[:5])
                with nc.Fori(0, HP // 2) as it:
                    with nc.Block() as block:
                        @block.tensor
                        def _(pe):
                            for j in range(2):
                                pe.wait_ge(pair_ready, 4 * (j + 1))
                                for c in range(NCH):
                                    n = j * NCH + c
                                    if n >= 4:
                                        pe.wait_ge(k_free, n - 3)
                                    for i in range(CH):
                                        r = c * CH + i
                                        mm = pe.matmul(banks[n % 4][:, i * P:(i + 1) * P], k_r[:, r, :],
                                                       epair[:, j, 0, :, S - 1 - r:2 * S - 1 - r], start=True, stop=True)
                                    mm.then_inc(k_full, 1)
                                for c in range(NCH):
                                    n = j * NCH + c
                                    if n >= 4:
                                        pe.wait_ge(q_free, n - 3)
                                    for i in range(CH):
                                        l = c * CH + i
                                        mm = pe.matmul(banks[4 + n % 4][:, i * P:(i + 1) * P], q_l[:, l, :],
                                                       epair[:, j, 1, :, S - 1 - l:2 * S - 1 - l], start=True, stop=True)
                                    mm.then_inc(q_full, 1)

                        @block.scalar
                        def _(act):
                            act.wait_ge(rel_stored, it * (16 * NCH) + 1)
                            for j in range(2):
                                for c in range(NCH):
                                    n = j * NCH + c
                                    act.wait_ge(k_full, n + 1)
                                    src = banks[n % 4].rearrange("p (r h l) -> p r h l", h=2, l=S)
                                    for h in range(2):
                                        ins = act.copy(rbuf[j][:, :, h, c * CH:(c + 1) * CH].rearrange("p l r -> p r l"), src[:, :, h, :])
                                    ins.then_inc(k_free, 1)

                        @block.vector
                        def _(dve):
                            for j in range(2):
                                for way in range(2):
                                    for h in range(2):
                                        dve.tensor_scalar(epair[:, j, way, h, :], emb[:, way, :],
                                                          W["head16"][:, bass.ds(it * 4 + (2 * j + h), 1)], None,
                                                          ALU.mult).then_inc(pair_ready, 1)
                            for j in range(2):
                                dve.wait_ge(k_free, (j + 1) * NCH)
                                for c in range(NCH):
                                    n = j * NCH + c
                                    dve.wait_ge(q_full, n + 1)
                                    part = rbuf[j][:, c * CH:(c + 1) * CH, :, :].rearrange("p l h r -> p (l h r)")
                                    dve.tensor_tensor(part, banks[4 + n % 4], part, ALU.add).then_inc(q_free, 1)

                        @block.sync
                        def _(sp):
                            for j in range(2):
                                for c in range(NCH // 2):
                                    sp.wait_ge(q_free, j * NCH + 2 * c + 2)
                                    sp.dma_start(
                                        rel[:, 2 * c * CH:2 * (c + 1) * CH, bass.ds((it * 2 + j) * 2, 2), :],
                                        rbuf[j][:, 2 * c * CH:2 * (c + 1) * CH, :, :]).then_inc(rel_stored, 16)
                    nc.all_engine_barrier(sems_to_clear=turn_sems)

        plan = psum_plan()

        def gs(name, shape, dt=F32):
            return [sb(f"{name}{g}", shape, dt) for g in range(G)]

        x_in = gs("x_in", [P, D])
        c_in = gs("c_in", [P, D])
        rel_in = gs("rel_in", [P, H16 * S])
        xT = gs("xT", [P, P])
        cT = gs("cT", [P, P + 1])
        x_a, x_b = gs("x_a", [P, D]), gs("x_b", [P, D])
        xb = gs("xb", [P, D])
        qk_sb = gs("qk_sb", [P, 4, P])
        qm = gs("qm", [P, 4, P])
        kbd = gs("kbd", [P, 2, 2, 4, S])
        v16 = gs("v16", [P, 2, HP, 2, D8 + 1])
        v32 = gs("v32", [P, 2, H8 // 2, 2, D32 + 1])
        probs = gs("probs", [P, H16 * S])
        probsT = gs("probsT", [P, HP, P])
        rmax = gs("rmax", [P, H16])
        att = gs("att", [P, 2 * P])
        attT = gs("attT", [P, 2, P])
        latT = gs("latT", [LAT, P])
        hbuf = gs("hbuf", [P, D])
        stat = gs("stat", [P, 6])
        mv = gs("mv", [P, 2])
        rstd = gs("rstd", [P, 2])
        x_out = gs("x_out", [P, D])
        q_tok = gs("q_tok", [P, P])
        pos = gs("pos", [P, NS])
        posi = gs("posi", [P, NS], I32)
        pw = gs("pw", [P, 4, NS])
        dist = gs("dist", [P, 2, NS])
        hat = gs("hat", [P, HP * NK, 2, 2])
        idx = gs("idx", [P, 2, 81])
        idxT = gs("idxT", [81, 2, P], F16)
        onehot = gs("onehot", [P, HP * NK, P], BF16)
        kv = gs("kv", [P, UNITS])
        kvc = gs("kvc", [P, 3, UNITS], BF16)
        table = gs("table", [P, 3, 2, UNITS], BF16)
        small = gs("small", [P, 3, NS])
        hT = gs("hT", [P, UNITS])

        bigp = gs("bigp", [P, NS * 2 * D8])
        wts = gs("wts", [P, 2 * NS])
        ranks = gs("ranks", [P, E * E])
        lc = gs("lc", [P, 3])
        samp = gs("samp", [P, HP * NK * 2, 32])

        def after(eng, name, g, k=None):
            per = SIGNALS[name]
            eng.wait_ge(sig[name], g * per + (per if k is None else k))

        def await_reader(pe, use):
            name, g = use
            who = READ_BY[name]
            if isinstance(who, tuple):
                after(pe, who[0], g, who[1])
            else:
                after(pe, who, g)

        def fullM(eng, name, g):
            s, n, _ = plan["M"][(name, g)]
            eng.wait_ge(m_full[s], n + 1)
            return psM[:, s, :]

        def takeM(pe, name, g):
            s, _, before = plan["M"][(name, g)]
            if before:
                await_reader(pe, before)
            return psM[:, s, :], m_full[s]

        def fullS(eng, name, g):
            s, n, _ = plan["S"][(name, g)]
            eng.wait_ge(s_full[s], n + 1)
            return psS[:, s, :]

        def takeS(pe, name, g):
            s, _, before = plan["S"][(name, g)]
            if before:
                await_reader(pe, before)
            return psS[:, s, :], s_full[s]

        heads_of = {"a0": (H16, D8), "a1": (H8, D32), "a2": (H16, D8)}
        x_of = {"a0": x_in, "g0": x_a, "f0": x_b, "a1": x_a, "a2": x_b, "f1": x_a}
        x_to = {"a0": x_a, "g0": x_b, "f0": x_a, "a1": x_b, "a2": x_a, "f1": x_out}
        x_ready = {"g0": "a0_x", "f0": "g0_x", "a1": "f0_x", "a2": "a1_x", "f1": "a2_x"}
        wo_of = {"a0": "a0_wo", "g0": "g0_wo", "a1": "a1_wo", "a2": "a2_wo"}

        all_rel = 16 * (S // 8) * HP + 1
        with nc.Block() as block:
            @block.vector
            def _(dve):
                dve.wait_ge(rel_stored, all_rel)
                for g in range(G):
                    dve.memset(v16[g][:], 0.0).then_inc(dve_step, 1)
                    dve.memset(v32[g][:], 0.0).then_inc(dve_step, 1)
                    dve.wait_ge(dve_step, 2 * g + 2)
                    for p in range(2):
                        r = slice(S * p, S * p + S)
                        dve.memset(v16[g][r, :, :, p, D8:D8 + 1], 1.0)
                        dve.memset(v32[g][r, :, :, p, D32:D32 + 1], 1.0)
                    dve.memset(idx[g][:, :, 80:81], 1.0)
                    dve.memset(cT[g][:, P:P + 1], 0.0)

            @block.gpsimd
            def _(pool):
                pool.wait_ge(rel_stored, all_rel)
                for g in range(G):
                    pool.memset(table[g][:], 0.0).then_inc(pool_step, 1)

            @block.sync
            def _(sp):
                sp.wait_ge(rel_stored, all_rel)
                for g in range(G):
                    for dst, src in ((x_in, x_t), (c_in, ctx_t), (rel_in, rel_t)):
                        sp.dma_start(dst[g][:, :], src[g]).then_inc(tiles_loaded, 16)
        nc.all_engine_barrier(sems_to_clear=turn_sems)

        with nc.Fori(0, TURNS) as it:
            with nc.Block() as block:
                @block.sync
                def _(sp):
                    for g in range(G):
                        after(sp, "a0_x", g)
                        nt = ((it + 1) % TURNS) * G + g
                        for dst, src in ((x_in, x_t), (c_in, ctx_t), (rel_in, rel_t)):
                            sp.dma_start(dst[g][:, :], src[bass.ds(nt, 1)].rearrange("o p d -> (o p) d")).then_inc(tiles_loaded, 16)
                    for g in range(G):
                        after(sp, "out_x", g)
                        sp.dma_start(out_t[bass.ds(it * G + g, 1)].rearrange("o p d -> (o p) d"), x_out[g][:, :]).then_inc(
                            out_stored, 16)

                @block.tensor
                def _(pe):
                    def transpose_x(l, g):
                        if l in x_ready:
                            after(pe, x_ready[l], g)
                        elif g == 0:
                            pe.wait_ge(tiles_loaded, (it + 1) * (16 * 3 * G))
                        ps, full = takeM(pe, f"{l}_xT", g)
                        mm = pe.transpose(ps[:, 0:P], x_of[l][g][:, :], ident[:, :])
                        if l == "a0":
                            mm = pe.transpose(ps[:, P:2 * P], c_in[g][:, :], ident[:, :])
                        mm.then_inc(full, 1)

                    def qkv(l, g):
                        after(pe, f"{l}_xT", g)
                        if l == "a0":
                            after(pe, "a0_cT", g)
                        ps, full = takeM(pe, f"{l}_qk", g)
                        if l == "a1":
                            after(pe, "a1_latent", g)
                            for c in range(2):
                                pe.matmul(ps[:, c * P:(c + 1) * P], W["a1_wq"][:, c * P:(c + 1) * P], xT[g][:, :],
                                          start=True, stop=True)
                                mm = pe.matmul(ps[:, (2 + c) * P:(3 + c) * P], W["a1_wk"][:, c * P:(c + 1) * P],
                                               latT[g][:, :], start=True, stop=True)
                            vin, vw, vk = latT[g], W["a1_wv"], 2 * S
                        else:
                            kin = xT[g][:, :] if l == "a0" else cT[g][:, 0:P]
                            pe.matmul(ps[:, 0:P], W[f"{l}_wq"][:, :], xT[g][:, :], start=True, stop=True)
                            mm = pe.matmul(ps[:, P:2 * P], W[f"{l}_wk"][:, :], kin, start=True, stop=True)
                            vin, vw, vk = (xT if l == "a0" else cT)[g], W[f"{l}_wv"], S
                        mm.then_inc(full, 1)
                        ps, full = takeM(pe, f"{l}_v", g)
                        for b in range(2):
                            for p in range(2):
                                mm = pe.matmul(ps[S * p:S * p + S, b * vk:(b + 1) * vk], vin[:, b * S:(b + 1) * S],
                                               vw[:, p * vk:(p + 1) * vk], start=True, stop=True)
                        mm.then_inc(full, 1)

                    def scores(l, g):
                        after(pe, f"{l}_masked", g)
                        ps, full = takeS(pe, f"{l}_scores", g)
                        for b in range(2):
                            for c in range(2 if l == "a1" else 4):
                                lhs = (qk_sb[g] if l == "a1" else qm[g])[:, c, b * S:(b + 1) * S]
                                rhs = kbd[g][:, c if l == "a1" else 0, b, :, :].rearrange("p h r -> p (h r)")
                                mm = pe.matmul(ps[b * S:(b + 1) * S, c * 256:(c + 1) * 256], lhs, rhs, start=True, stop=True)
                        mm.then_inc(full, 1)

                    def transpose_probs(l, g):
                        after(pe, f"{l}_probs", g)
                        for c in range(1 if l == "a1" else 2):
                            ps, full = takeM(pe, f"{l}_pT{c}", g)
                            for i in range(4):
                                n = 4 * c + i
                                mm = pe.transpose(ps[:, i * P:(i + 1) * P], probs[g][:, n * P:(n + 1) * P], ident[:, :])
                            mm.then_inc(full, 1)

                    def probs_values(l, g):
                        heads, d = heads_of[l]
                        after(pe, f"{l}_probsT0", g)
                        if l != "a1":
                            after(pe, f"{l}_probsT1", g)
                        after(pe, f"{l}_v", g)
                        ps, full = takeM(pe, f"{l}_pv", g)
                        v = v32[g] if l == "a1" else v16[g]
                        w = 2 * (d + 1)
                        for n in range(heads // 2):
                            for b in range(2):
                                mm = pe.matmul(ps[b * S:(b + 1) * S, n * w:(n + 1) * w],
                                               probsT[g][:, n, b * S:(b + 1) * S],
                                               v[:, b, n, :, :].rearrange("p h d -> p (h d)"), start=True, stop=True)
                        mm.then_inc(full, 1)

                    def transpose_ctx(l, g):
                        after(pe, f"{l}_ctx", g)
                        ps, full = takeM(pe, f"{l}_cT", g)
                        for c in range(2 if l == "a1" else 1):
                            mm = pe.transpose(ps[:, c * P:(c + 1) * P], att[g][:, c * P:(c + 1) * P], ident[:, :])
                        mm.then_inc(full, 1)

                    def project(l, g):
                        after(pe, f"{l}_ctxT", g)
                        ps, full = takeM(pe, f"{l}_o", g)
                        n = 2 if l == "a1" else 1
                        for c in range(n):
                            mm = pe.matmul(ps[:, 0:D], attT[g][:, c, :], W[wo_of[l]][:, c * D:(c + 1) * D],
                                           start=(c == 0), stop=(c == n - 1))
                        mm.then_inc(full, 1)

                    def latent(g):
                        after(pe, "a1_xT", g)
                        ps, full = takeM(pe, "a1_lat", g)
                        pe.matmul(ps[0:LAT, 0:P], W["a1_wkv"][:, :], xT[g][:, :], start=True, stop=True).then_inc(full, 1)

                    def sample_inputs(g):
                        after(pe, "g0_xT", g)
                        ps, full = takeM(pe, "g0_q", g)
                        pe.matmul(ps[:, 0:P], W["g0_wq"][:, :], xT[g][:, :], start=True, stop=True)
                        pe.matmul(ps[:, P:2 * P], xT[g][:, :], W["g0_wq"][:, :], start=True, stop=True).then_inc(full, 1)
                        ps, full = takeM(pe, "g0_kv", g)
                        dst = ps.rearrange("p (b n e w) -> p b e n w", b=2, n=HP, e=2)
                        for b in range(2):
                            for e in range(2):
                                for p in range(2):
                                    mm = pe.matmul(dst[S * p:S * p + S, b, e, :, :], cT[g][:, b * S + e:(b + 1) * S + e],
                                                   W["g0_wkv"][:, p * P:(p + 1) * P], start=True, stop=True)
                        mm.then_inc(full, 1)

                    def offsets(g):
                        after(pe, "g0_qT", g)
                        ps, full = takeM(pe, "g0_off", g)
                        pe.matmul(ps[:, 0:NS], qk_sb[g][:, 0, :], W["g0_woff"][:, :], start=True, stop=True).then_inc(full, 1)

                    def transpose_idx(g):
                        after(pe, "g0_idx", g)
                        ps, full = takeM(pe, "g0_idxT", g)
                        for c in range(2):
                            mm = pe.transpose(ps[0:81, c * P:(c + 1) * P], idx[g][:, c, :], ident[:, :])
                        mm.then_inc(full, 1)

                    def spread_idx(g):
                        after(pe, "g0_idxT", g)
                        for u in range(10):
                            ps, full = takeM(pe, f"g0_eq{u}", g)
                            for i in range(4):
                                half, n = divmod(4 * u + i, 20)
                                mm = pe.matmul(ps[:, i * P:(i + 1) * P], W["spread"][:, n * P:(n + 1) * P],
                                               idxT[g][:, half, :], start=True, stop=True)
                            mm.then_inc(full, 1)

                    def sample(g):
                        after(pe, "g0_table", g)
                        after(pe, "g0_onehotA", g)
                        after(pe, "g0_onehotV", g)
                        for n in range(HP):
                            ps, full = takeM(pe, f"g0_s{n}", g)
                            for b in range(2):
                                for k in range(NK):
                                    for part in range(3):
                                        rhs = table[g][:, part, :, (b * HP + n) * 32:(b * HP + n + 1) * 32].rearrange(
                                            "p h (w d) -> p w h d", d=D8)
                                        mm = pe.matmul(ps[b * S:(b + 1) * S, k * 64:(k + 1) * 64],
                                                       onehot[g][:, n * NK + k, b * S:(b + 1) * S], rhs,
                                                       start=(part == 0), stop=(part == 2))
                            mm.then_inc(full, 1)

                    def router(g):
                        after(pe, "f0_xT", g)
                        ps, full = takeM(pe, "f0_lg", g)
                        pe.matmul(ps[:, 0:2 * E], xT[g][:, :], c_normT[:, :], start=True, stop=True).then_inc(full, 1)
                        ps, full = takeM(pe, "f0_h", g)
                        for c in range(4):
                            mm = pe.matmul(ps[:, c * P:(c + 1) * P], W["f0_w1"][:, c * P:(c + 1) * P], xT[g][:, :],
                                           start=True, stop=True)
                        mm.then_inc(full, 1)

                    def transpose_gates(g):
                        after(pe, "f0_gates", g)
                        ps, full = takeM(pe, "f0_gT", g)
                        pe.transpose(ps[0:E, 0:P], small[g][:, 0, 0:E], ident[:, :]).then_inc(full, 1)

                    def spread_gates(g):
                        after(pe, "f0_gatesT", g)
                        ps, full = takeM(pe, "f0_gb", g)
                        for c in range(4):
                            mm = pe.matmul(ps[:, c * P:(c + 1) * P], W["expert_rows"][:, c * P:(c + 1) * P],
                                           latT[g][0:E, :], start=True, stop=True)
                        mm.then_inc(full, 1)

                    def experts_out(g):
                        after(pe, "f0_gated", g)
                        ps, full = takeM(pe, "f0_o", g)
                        for c in range(4):
                            pe.matmul(ps[:, 0:D], hT[g][:, c * P:(c + 1) * P], W["f0_w2"][:, c * D:(c + 1) * D],
                                      start=(c == 0), stop=False)
                        pe.matmul(ps[:, 0:D], latT[g][0:E, :], W["f0_b2"][:, :], start=False, stop=True).then_inc(full, 1)

                    def experts1(g):
                        after(pe, "f1_xT", g)
                        ps, full = takeM(pe, "f1_gs", g)
                        pe.matmul(ps[:, 0:E], xT[g][:, :], W["f1_gw"][:, :], start=True, stop=True).then_inc(full, 1)
                        ps, full = takeS(pe, "f1_y", g)
                        for c in range(2):
                            o = ps[:, c * UNITS:(c + 1) * UNITS]
                            pe.matmul(o, xT[g][:, :], W["f1_w"][:, c * UNITS:(c + 1) * UNITS], start=True, stop=False)
                            mm = pe.matmul(o, W["ones_row"][:, :], W["f1_b"][:, c * UNITS:(c + 1) * UNITS], start=False, stop=True)
                        mm.then_inc(full, 1)

                    run = {"g0_B": sample_inputs, "g0_C": offsets, "g0_D": transpose_idx, "g0_E": spread_idx, "g0_F": sample,
                           "f0_B": router, "f0_C": transpose_gates, "f0_D": spread_gates, "f0_E": experts_out,
                           "a1_L": latent, "f1_B": experts1}
                    for stage in STAGES:
                        l, s = stage.split("_")
                        for g in range(G):
                            if stage in run:
                                run[stage](g)
                            elif s == "A":
                                transpose_x(l, g)
                            elif (l, s) in (("g0", "G"),):
                                transpose_ctx(l, g)
                            elif (l, s) in (("g0", "H"),):
                                project(l, g)
                            else:
                                {"B": qkv, "C": scores, "D": transpose_probs, "E": probs_values, "F": transpose_ctx,
                                 "G": project}[s](l, g)

                @block.scalar
                def _(act):
                    def copy_xT(l, g):
                        ps = fullM(act, f"{l}_xT", g)
                        ins = act.copy(xT[g][:, :], ps[:, 0:P])
                        ins.then_inc(sig[f"{l}_xT"], 1)
                        if l == "a0":
                            ins = act.copy(cT[g][:, 0:P], ps[:, P:2 * P])
                            ins.then_inc(sig["a0_cT"], 1)
                            after(act, "a0_cT", g)

                    def copy_qk(l, g):
                        ps = fullM(act, f"{l}_qk", g)
                        if l == "a1":
                            act.copy(qk_sb[g][:, 0:2, :].rearrange("p c q -> p (c q)"), ps[:, 0:2 * P]).then_inc(sig["a1_qk"], 1)
                            act.copy(qk_sb[g][:, 2:4, :].rearrange("p c q -> p (c q)"), ps[:, 2 * P:4 * P]).then_inc(sig["a1_qk"], 1)
                        else:
                            act.activation(qk_sb[g][:, 0, :], ps[:, 0:P], ACT.Identity,
                                           bias=W[f"{l}_bq"][:, 0:1]).then_inc(sig[f"{l}_qk"], 1)
                            act.activation(qk_sb[g][:, 1, :], ps[:, P:2 * P], ACT.Identity,
                                           bias=W[f"{l}_bk"][:, 0:1]).then_inc(sig[f"{l}_qk"], 1)

                    def exponential(l, g):
                        n = heads_of[l][0] * S
                        after(act, f"{l}_shifted", g)
                        act.activation(probs[g][:, 0:n], probs[g][:, 0:n], ACT.Exp,
                                       scale=R32 if l == "a1" else R8).then_inc(sig[f"{l}_probs"], 1)

                    def copy_probsT(l, g):
                        ps = fullM(act, f"{l}_pT0", g)
                        act.copy(probsT[g][:, 0:4, :].rearrange("p n q -> p (n q)"), ps).then_inc(sig[f"{l}_probsT0"], 1)

                    def copy_ctxT(l, g):
                        ps = fullM(act, f"{l}_cT", g)
                        n = 2 if l == "a1" else 1
                        act.copy(attT[g][:, 0:n, :].rearrange("p c q -> p (c q)"), ps[:, 0:n * P]).then_inc(sig[f"{l}_ctxT"], 1)

                    def latent(g):
                        ps = fullM(act, "a1_lat", g)
                        act.copy(latT[g][:, :], ps[0:LAT, 0:P]).then_inc(sig["a1_latent"], 1)

                    def high_parts(g):
                        after(act, "g0_kv", g)
                        act.copy(kvc[g][:, 0, :], kv[g][:, :]).then_inc(sig["g0_hi"], 1)
                        after(act, "g0_rest", g)
                        act.copy(kvc[g][:, 1, :], kv[g][:, :]).then_inc(sig["g0_mid"], 1)

                    def hats(g):
                        after(act, "g0_dist", g)
                        act.activation(dist[g][:, :, :], dist[g][:, :, :], ACT.Abs).then_inc(sig["g0_hat"], 1)

                    def idxT_copy(g):
                        ps = fullM(act, "g0_idxT", g)
                        act.copy(idxT[g][:, :, :].rearrange("p c q -> p (c q)"), ps[0:81, 0:2 * P]).then_inc(sig["g0_idxT"], 1)

                    def onehots(g):
                        for u in range(10):
                            if ONEHOT_BY[u] == "A":
                                ps = fullM(act, f"g0_eq{u}", g)
                                act.activation(onehot[g][:, 4 * u:4 * u + 4, :].rearrange("p n q -> p (n q)"), ps,
                                               ACT.Relu).then_inc(sig["g0_onehotA"], 1)

                    def copy_samples(g):
                        for n in range(HP):
                            ps = fullM(act, f"g0_s{n}", g)
                            act.copy(samp[g][:, n * 10:(n + 1) * 10, :].rearrange("p n w -> p (n w)"), ps[:, 0:NK * 64]).then_inc(
                                sig["g0_sampled"], 1)

                    def sample_exp(g):
                        after(act, "g0_shifted", g)
                        act.activation(small[g][:, 1, :], small[g][:, 1, :], ACT.Exp, scale=0.5 * R8).then_inc(sig["g0_probs"], 1)

                    def logits(g):
                        ps = fullM(act, "f0_lg", g)
                        act.copy(small[g][:, 2, 0:2 * E], ps[:, 0:2 * E]).then_inc(sig["f0_logits"], 1)
                        ps = fullM(act, "f0_h", g)
                        for c in range(4):
                            act.activation(hT[g][:, c * P:(c + 1) * P], ps[:, c * P:(c + 1) * P], ACT.Gelu,
                                           bias=W["f0_b1"][:, c:c + 1]).then_inc(sig["f0_h"], 1)

                    def gate_exp(g):
                        after(act, "f0_shifted", g)
                        act.activation(small[g][:, 1, 0:E], small[g][:, 1, 0:E], ACT.Exp).then_inc(sig["f0_exp"], 1)

                    def gatesT(g):
                        ps = fullM(act, "f0_gT", g)
                        act.copy(latT[g][0:E, :], ps[0:E, 0:P]).then_inc(sig["f0_gatesT"], 1)

                    def gate1_exp(g):
                        after(act, "f1_shifted", g)
                        act.activation(small[g][:, 1, 0:E], small[g][:, 1, 0:E], ACT.Exp).then_inc(sig["f1_exp"], 1)

                    run = {"g0_B": [high_parts], "g0_C": [hats], "g0_D": [idxT_copy], "g0_E": [onehots],
                           "g0_F": [copy_samples], "f0_B": [logits], "f0_C": [gatesT], "a1_L": [latent], "f1_B": [gate1_exp],
                           "f0_D": [], "f0_E": [], "g0_H": []}
                    for stage in STAGES:
                        l, s = stage.split("_")
                        if stage == "g0_G":
                            for g in range(G):
                                sample_exp(g)
                        if stage == "f0_C":
                            for g in range(G):
                                gate_exp(g)
                        for g in range(G):
                            if stage in run:
                                for f in run[stage]:
                                    f(g)
                            elif s == "A":
                                copy_xT(l, g)
                            elif stage == "g0_G":
                                copy_ctxT(l, g)
                            elif s in "BCDF":
                                {"B": copy_qk, "C": exponential, "D": copy_probsT, "F": copy_ctxT}[s](l, g)

                @block.vector
                def _(dve):
                    steps = [0]

                    def link(ins):
                        steps[0] += 1
                        ins.then_inc(dve_step, 1)
                        dve.wait_ge(dve_step, steps[0])

                    def bc(name, n=D):
                        return W["bc_" + name][:, 0:n]

                    def values(l, g):
                        heads, d = heads_of[l]
                        ps = fullM(dve, f"{l}_v", g)
                        v = v32[g] if l == "a1" else v16[g]
                        n = heads // 2
                        for p in range(2):
                            r = slice(S * p, S * p + S)
                            src = ps[r, 0:2 * n * d].rearrange("p (b n d) -> p b n d", b=2, n=n)
                            if l == "a1":
                                ins = dve.tensor_copy(v[r, :, :, p, 0:d], src)
                            else:
                                bias = spread(W[f"bc_{l}_bv"][r, :].rearrange("p (n d) -> p n d", n=n), 1, 2)
                                ins = dve.tensor_tensor(v[r, :, :, p, 0:d], src, bias, ALU.add)
                            ins.then_inc(sig[f"{l}_v"], 1)

                    def shift(l, g):
                        heads = heads_of[l][0]
                        n = heads * S
                        ps = fullS(dve, f"{l}_scores", g)
                        pr = probs[g][:, 0:n]
                        pr3 = pr.rearrange("p (h r) -> p h r", r=S)
                        src = ps[:, 0:n]
                        if l == "a0":
                            dve.tensor_tensor(pr, src, rel_in[g][:, :], ALU.add).then_inc(sig["a0_summed"], 1)
                            after(dve, "a0_summed", g)
                            src = pr
                        if l == "a2":
                            m = spread(mask01[:, :], 1, heads)
                            mn = spread(maskneg[:, :], 1, heads)
                            dve.tensor_tensor(pr3, src.rearrange("p (h r) -> p h r", r=S), m, ALU.mult).then_inc(sig["a2_where"], 1)
                            after(dve, "a2_where", g)
                            link(dve.tensor_tensor(pr3, pr3, mn, ALU.add))
                            src = pr
                        link(dve.tensor_reduce(rmax[g][:, 0:heads], src.rearrange("p (h r) -> p h r", r=S), AX, ALU.max))
                        dve.tensor_tensor(pr3, src.rearrange("p (h r) -> p h r", r=S),
                                          spread(rmax[g][:, 0:heads], 2, S),
                                          ALU.subtract).then_inc(sig[f"{l}_shifted"], 1)

                    def copy_probsT(l, g):
                        if l != "a1":
                            ps = fullM(dve, f"{l}_pT1", g)
                            dve.tensor_copy(probsT[g][:, 4:8, :], ps.rearrange("p (n q) -> p n q", n=4)).then_inc(
                                sig[f"{l}_probsT1"], 1)

                    def normalise(l, g):
                        heads, d = heads_of[l]
                        ps = fullM(dve, f"{l}_pv", g)
                        o = ps[:, 0:heads * (d + 1)].rearrange("p (h d) -> p h d", h=heads)
                        link(dve.reciprocal(rmax[g][:, 0:heads].unsqueeze(2), o[:, :, d:d + 1]))
                        dve.tensor_tensor(att[g][:, 0:heads * d].rearrange("p (h d) -> p h d", h=heads), o[:, :, 0:d],
                                          spread(rmax[g][:, 0:heads], 2, d), ALU.mult).then_inc(sig[f"{l}_ctx"], 1)

                    def norm(name, g, dst, done):
                        link(dve.bn_stats(stat[g][:, :], hbuf[g][:, :]))
                        dve.bn_aggr(mv[g][:, :], stat[g][:, :]).then_inc(sig[f"{name}_var"], 1)
                        after(dve, f"{name}_rstd", g)
                        return dve.tensor_scalar(dst, hbuf[g][:, :], mv[g][:, 0:1], rstd[g][:, 1:2], ALU.subtract, ALU.mult)

                    def residual(l, g):
                        ps = fullM(dve, f"{l}_o", g)
                        add = x_of[l][g][:, :] if l in ("a1", "f0") else xb[g][:, :]
                        if l in ("a0", "g0", "a2"):
                            after(dve, f"{l}_xb", g)
                        dve.tensor_tensor(hbuf[g][:, :], ps[:, 0:D], add, ALU.add).then_inc(sig[f"{l}_added"], 1)
                        after(dve, f"{l}_added", g)
                        if l == "a0":
                            link(norm("a0i", g, hbuf[g][:, :], None))
                            link(dve.tensor_tensor(hbuf[g][:, :], hbuf[g][:, :], bc("a0_gamma"), ALU.mult))
                            link(dve.tensor_tensor(hbuf[g][:, :], hbuf[g][:, :], bc("a0_beta"), ALU.add))
                            link(dve.tensor_tensor(hbuf[g][:, :], hbuf[g][:, :], x_in[g][:, :], ALU.add))
                        norm(l, g, x_to[l][g][:, :], None).then_inc(sig[f"{l}_x"], 1)
                        after(dve, f"{l}_x", g)

                    def sample_inputs(g):
                        ps = fullM(dve, "g0_q", g)
                        dve.tensor_scalar(qk_sb[g][:, 0, :], ps[:, 0:P], W["g0_bq"][:, 0:1], None, ALU.add).then_inc(sig["g0_qT"], 1)
                        dve.tensor_tensor(q_tok[g][:, :], ps[:, P:2 * P], bc("g0_bq"), ALU.add).then_inc(sig["g0_qtok"], 1)
                        ps = fullM(dve, "g0_kv", g)
                        dve.tensor_tensor(kv[g][:, :].rearrange("p (n w) -> p n w", n=2 * HP), ps.rearrange("p (n w) -> p n w", n=2 * HP),
                                          bc("g0_bkv", UNITS).rearrange("p (n w) -> p n w", n=2 * HP), ALU.add).then_inc(sig["g0_kv"], 1)

                    def split_parts(g):
                        after(dve, "g0_hi", g)
                        dve.tensor_tensor(kv[g][:, :], kv[g][:, :], kvc[g][:, 0, :], ALU.subtract).then_inc(sig["g0_rest"], 1)
                        after(dve, "g0_mid", g)
                        link(dve.tensor_tensor(kvc[g][:, 2, :], kv[g][:, :], kvc[g][:, 1, :], ALU.subtract))
                        for p in range(2):
                            r = slice(S * p, S * p + S)
                            for part in range(3):
                                dve.tensor_copy(table[g][r, part, p, :], kvc[g][r, part, :]).then_inc(sig["g0_table"], 1)

                    def positions(g):
                        ps = fullM(dve, "g0_off", g)
                        dve.scalar_tensor_tensor(out=pos[g][:, :], in0=ps[:, 0:NS], scalar=W["query_pos"][:, 0:1],
                                                 in1=bc("off", NS), op0=ALU.add, op1=ALU.add).then_inc(sig["g0_pos"], 1)

                    def onehots(g):
                        for u in range(10):
                            if ONEHOT_BY[u] == "V":
                                ps = fullM(dve, f"g0_eq{u}", g)
                                dve.tensor_scalar(onehot[g][:, 4 * u:4 * u + 4, :].rearrange("p n q -> p (n q)"), ps, 0.0,
                                                  None, ALU.max).then_inc(sig["g0_onehotV"], 1)

                    def hat_weights(g):
                        after(dve, "g0_hat", g)
                        for e in range(2):
                            link(dve.tensor_scalar(hat[g][:, :, e, :], dist[g][:, e, :].rearrange("p (n h) -> p n h", h=2),
                                                   -1.0, 1.0, ALU.mult, ALU.add))
                        hh = hat[g][:, :, :, :].rearrange("p n e h -> p (n e h)")
                        link(dve.tensor_scalar(hh, hh, 0.0, None, ALU.max))

                    def sampled_attention(g):
                        n40 = HP * NK
                        after(dve, "g0_sampled", g)
                        after(dve, "g0_qtok", g)
                        sm = samp[g]
                        kp = bigp[g][:, :].rearrange("p (n k w) -> p n k w", n=HP, k=2 * NK)
                        kin = sm[:, :, 0:16].rearrange("p (n k) w -> p n k w", n=HP)
                        q4 = spread(q_tok[g][:, :].rearrange("p (n w) -> p n w", n=HP), 2, 2 * NK)
                        link(dve.tensor_tensor(kp, kin, q4, ALU.mult))
                        sc = wts[g]
                        link(dve.tensor_reduce(sc[:, :], bigp[g][:, :].rearrange("p (n d) -> p n d", d=D8), AX, ALU.add))
                        hh = hat[g][:, :, :, :].rearrange("p n e h -> p (n e h)")
                        link(dve.tensor_tensor(sc[:, :], sc[:, :], hh, ALU.mult))
                        sv = sc[:, :].rearrange("p (n e h) -> p n e h", e=2, h=2)
                        s1 = small[g][:, 1, :]
                        s1n = s1.rearrange("p (n h) -> p n h", h=2)
                        link(dve.tensor_tensor(s1n, sv[:, :, 0, :], sv[:, :, 1, :], ALU.add))
                        by_head = s1.rearrange("p (n k h) -> p n h k", n=HP, h=2)
                        mx = rmax[g][:, :].rearrange("p (n h) -> p n h", h=2)
                        link(dve.tensor_reduce(mx, by_head, AX, ALU.max))
                        k3 = s1.rearrange("p (n k h) -> p n k h", n=HP, h=2)
                        mxb = spread(mx, 2, NK)
                        dve.tensor_tensor(k3, k3, mxb, ALU.subtract).then_inc(sig["g0_shifted"], 1)
                        after(dve, "g0_probs", g)
                        link(dve.tensor_reduce(mx, by_head, AX, ALU.add))
                        link(dve.tensor_scalar(rmax[g][:, :], rmax[g][:, :], 2.0, None, ALU.mult))
                        link(dve.reciprocal(rmax[g][:, :], rmax[g][:, :]))
                        link(dve.tensor_tensor(k3, k3, mxb, ALU.mult))
                        link(dve.tensor_tensor(sv, hat[g][:, :, :, :],
                                               spread(s1n, 2, 2), ALU.mult))
                        vin = sm[:, :, 16:32].rearrange("p n (h d) -> p n h d", h=2)
                        wv = spread(sc[:, :].rearrange("p (n h) -> p n h", h=2), 3, D8)
                        link(dve.tensor_tensor(bigp[g][:, :].rearrange("p (n h d) -> p n h d", h=2, d=D8), vin, wv, ALU.mult))
                        dve.tensor_reduce(att[g][:, 0:P].rearrange("p (n w) -> p n w", n=HP),
                                          bigp[g][:, :].rearrange("p (n k w) -> p n w k", n=HP, k=2 * NK), AX, ALU.add).then_inc(sig["g0_ctx"], 1)

                    def squares(g):
                        link(dve.tensor_tensor(hbuf[g][:, :], x_b[g][:, :], x_b[g][:, :], ALU.mult))
                        dve.tensor_reduce(rstd[g][:, 0:1], hbuf[g][:, :], AX, ALU.add).then_inc(sig["f0_sq"], 1)

                    def route(g):
                        lg = small[g][:, 2, :]
                        after(dve, "f0_rnorm", g)
                        after(dve, "f0_logits", g)
                        link(dve.tensor_scalar(rstd[g][:, 0:1], rstd[g][:, 1:2], 1e12, None, ALU.min))
                        link(dve.scalar_tensor_tensor(out=lg[:, 16:24], in0=lg[:, 0:E], scalar=rstd[g][:, 0:1], in1=lg[:, E:2 * E],
                                                      op0=ALU.mult, op1=ALU.add))
                        link(dve.max(lg[:, 24:32], lg[:, 16:24]))
                        link(dve.tensor_scalar(lg[:, 32:40], lg[:, 16:24], lg[:, 25:26], None, ALU.is_ge))
                        dve.tensor_scalar(small[g][:, 1, 0:E], lg[:, 16:24], lg[:, 24:25], None, ALU.subtract).then_inc(sig["f0_shifted"], 1)
                        after(dve, "f0_exp", g)
                        link(dve.tensor_tensor(lg[:, 40:48], small[g][:, 1, 0:E], lg[:, 32:40], ALU.mult))
                        link(dve.tensor_reduce(lg[:, 48:49], lg[:, 40:48], AX, ALU.add))
                        link(dve.reciprocal(lg[:, 49:50], lg[:, 48:49]))
                        dve.tensor_scalar(small[g][:, 0, 0:E], lg[:, 40:48], lg[:, 49:50], None, ALU.mult).then_inc(sig["f0_gates"], 1)

                    def gate_hidden(g):
                        ps = fullM(dve, "f0_gb", g)
                        after(dve, "f0_h", g)
                        dve.tensor_tensor(hT[g][:, :], hT[g][:, :], ps, ALU.mult).then_inc(sig["f0_gated"], 1)

                    def mixture(g):
                        ps = fullM(dve, "f1_gs", g)
                        lg = small[g][:, 2, :]
                        dve.tensor_tensor(lg[:, 0:E], ps[:, 0:E], bc("f1_gb", E), ALU.add).then_inc(sig["f1_scored"], 1)
                        after(dve, "f1_scored", g)
                        link(dve.tensor_scalar(lg[:, 0:E], lg[:, 0:E], 1e-4, None, ALU.max))
                        link(dve.tensor_reduce(lg[:, 8:9], lg[:, 0:E], AX, ALU.max))
                        dve.tensor_scalar(small[g][:, 1, 0:E], lg[:, 0:E], lg[:, 8:9], None, ALU.subtract).then_inc(sig["f1_shifted"], 1)

                    def mixture_gates(g):
                        lg = small[g][:, 2, :]
                        after(dve, "f1_exp", g)
                        link(dve.tensor_reduce(lg[:, 9:10], small[g][:, 1, 0:E], AX, ALU.add))
                        link(dve.reciprocal(lg[:, 10:11], lg[:, 9:10]))
                        dve.tensor_scalar(lg[:, 16:24], small[g][:, 1, 0:E], lg[:, 10:11], None, ALU.mult).then_inc(sig["f1_p"], 1)

                    def mixture_out(g):
                        lg = small[g][:, 2, :]
                        after(dve, "f1_rank", g)
                        link(dve.tensor_reduce(lg[:, 24:32], ranks[g][:, :].rearrange("p (a b) -> p a b", a=E), AX, ALU.add))
                        link(dve.tensor_scalar(lg[:, 24:32], lg[:, 24:32], 2.0, None, ALU.is_lt))
                        link(dve.tensor_scalar(lg[:, 32:40], lg[:, 16:24], 0.1, None, ALU.max))
                        link(dve.tensor_tensor(lg[:, 32:40], lg[:, 32:40], lg[:, 24:32], ALU.mult))
                        link(dve.tensor_reduce(lg[:, 11:12], lg[:, 32:40], AX, ALU.add))
                        link(dve.reciprocal(lg[:, 12:13], lg[:, 11:12]))
                        link(dve.tensor_scalar(lg[:, 40:48], lg[:, 32:40], lg[:, 12:13], 0.5, ALU.mult, ALU.mult))
                        ps = fullS(dve, "f1_y", g)
                        dve.tensor_tensor(probs[g][:, :].rearrange("p (e f) -> p e f", e=E), ps.rearrange("p (e f) -> p e f", e=E),
                                          spread(lg[:, 40:48], 2, D), ALU.mult).then_inc(sig["f1_mixed"], 1)
                        after(dve, "f1_mixed", g)
                        link(dve.tensor_reduce(att[g][:, 0:D], probs[g][:, :].rearrange("p (e f) -> p f e", e=E), AX, ALU.add))
                        link(dve.tensor_tensor(hbuf[g][:, :], att[g][:, 0:D], x_a[g][:, :], ALU.add))
                        ins = norm("f1", g, x_out[g][:, :], None)
                        ins.then_inc(sig["out_x"], 1)

                    run = {"g0_B": [sample_inputs, split_parts], "g0_C": [positions], "g0_D": [hat_weights], "g0_E": [onehots],
                           "g0_F": [], "g0_G": [], "g0_H": [lambda g: residual("g0", g)],
                           "f0_A": [squares], "f0_B": [route], "f0_C": [], "f0_D": [gate_hidden], "f0_E": [lambda g: residual("f0", g)],
                           "a1_L": [], "f1_B": []}
                    for stage in STAGES:
                        l, s = stage.split("_")
                        if stage == "g0_G":
                            for g in range(G):
                                sampled_attention(g)
                            continue
                        if stage == "f1_B":
                            dve.wait_ge(out_stored, it * (16 * G) + 1)
                            for f in (mixture, mixture_gates, mixture_out):
                                for g in range(G):
                                    f(g)
                            continue
                        for g in range(G):
                            if stage in run:
                                for f in run[stage]:
                                    f(g)
                            elif s in "BCDEG":
                                {"B": values, "C": shift, "D": copy_probsT, "E": normalise, "G": residual}[s](l, g)

                @block.gpsimd
                def _(pool):
                    steps = [0]

                    def link(ins):
                        steps[0] += 1
                        ins.then_inc(pool_step, 1)
                        pool.wait_ge(pool_step, steps[0])

                    def masks(l, g):
                        after(pool, f"{l}_qk", g)
                        for c in range(4 if l != "a1" else 0):
                            pool.tensor_scalar(qm[g][:, c, :], qk_sb[g][:, 0, :], W["group4"][:, c:c + 1], None,
                                               ALU.mult).then_inc(sig[f"{l}_masked"], 1)
                        for t in range(2 if l == "a1" else 1):
                            src = qk_sb[g][:, 2 + t if l == "a1" else 1, :].rearrange("p (b r) -> p b r", b=2)
                            m = W["group4"] if l == "a1" else W["within4"]
                            for c in range(4):
                                pool.tensor_scalar(kbd[g][:, t, :, c, :], src, m[:, c:c + 1], None,
                                                   ALU.mult).then_inc(sig[f"{l}_masked"], 1)

                    def bias_residual(l, g):
                        if l in x_ready:
                            after(pool, x_ready[l], g)
                        pool.tensor_tensor(xb[g][:, :], x_of[l][g][:, :], W[f"bc_{l}_bo"][:, :], ALU.add).then_inc(sig[f"{l}_xb"], 1)

                    def rsqrt(name, g, eps):
                        after(pool, f"{name}_var", g)
                        link(pool.tensor_scalar(rstd[g][:, 0:1], mv[g][:, 1:2], eps, None, ALU.add))
                        pool.tensor_tensor(rstd[g][:, 1:2], rstd[g][:, 0:1], mhalf[:, :], ALU.pow).then_inc(sig[f"{name}_rstd"], 1)

                    def norms(l, g):
                        if l == "a0":
                            rsqrt("a0i", g, 1e-12)
                        rsqrt(l, g, EPS_LN)

                    def sampling_index(g):
                        t = bass.ds(it * G + g, 1)
                        after(pool, "g0_pos", g)
                        w = [pw[g][:, i, :] for i in range(4)]
                        L, Linv, Lpos = (lc[g][:, i:i + 1] for i in range(3))
                        link(pool.tensor_copy(L, lens[:, t]))
                        link(pool.tensor_copy(Linv, lens_inv[:, t]))
                        link(pool.tensor_copy(Lpos, lens_pos[:, t]))
                        link(pool.tensor_scalar(posi[g][:, :], pos[g][:, :], Linv, None, ALU.mult))
                        link(pool.tensor_scalar(w[0], posi[g][:, :], L, None, ALU.mult))
                        link(pool.tensor_tensor(w[1], pos[g][:, :], w[0], ALU.subtract))
                        link(pool.tensor_scalar(w[0], w[1], 0.0, Lpos, ALU.is_lt, ALU.mult))
                        link(pool.tensor_tensor(w[1], w[1], w[0], ALU.add))
                        link(pool.tensor_scalar(w[0], w[1], L, Lpos, ALU.is_ge, ALU.mult))
                        link(pool.tensor_tensor(w[1], w[1], w[0], ALU.subtract))
                        link(pool.tensor_scalar(w[2], w[1], float(S) / (S - 1), -0.5, ALU.mult, ALU.add))
                        link(pool.tensor_copy(posi[g][:, :], w[2]))
                        link(pool.tensor_copy(w[1], posi[g][:, :]))
                        link(pool.tensor_tensor(w[0], w[1], w[2], ALU.subtract))
                        link(pool.tensor_scalar(w[0], w[0], 0.0, None, ALU.is_gt))
                        link(pool.tensor_tensor(w[1], w[1], w[0], ALU.subtract))
                        link(pool.tensor_scalar(w[1], w[1], 0.0, float(S - 2), ALU.max, ALU.min))
                        i0 = idx[g][:, :, 0:40]
                        pool.tensor_scalar(i0, w[1].rearrange("p (a n) -> p a n", a=2), -32.0, None,
                                           ALU.add).then_inc(sig["g0_idx"], 1)
                        after(pool, "g0_idx", g, 1)
                        pool.tensor_tensor(idx[g][:, :, 40:80], i0, i0, ALU.mult).then_inc(sig["g0_idx"], 1)
                        link(pool.tensor_tensor(dist[g][:, 0, :], w[2], w[1], ALU.subtract))
                        pool.tensor_scalar(dist[g][:, 1, :], dist[g][:, 0, :], -1.0, None, ALU.add).then_inc(sig["g0_dist"], 1)

                    def ranks_of(g):
                        after(pool, "f1_p", g)
                        p = small[g][:, 2, 16:24]
                        other = spread(p, 1, E)
                        own = spread(p, 2, E)
                        r3 = ranks[g][:, :].rearrange("p (a b) -> p a b", a=E)
                        d3 = pw[g][:, 1, 0:64].rearrange("p (a b) -> p a b", a=E)
                        e3 = pw[g][:, 0, 0:64].rearrange("p (a b) -> p a b", a=E)
                        link(pool.tensor_tensor(d3, other, own, ALU.subtract))
                        link(pool.tensor_scalar(r3, d3, 0.0, None, ALU.is_gt))
                        link(pool.tensor_scalar(e3, d3, 0.0, None, ALU.is_equal))
                        link(pool.tensor_tensor(e3, e3, W["bc_lower"][:, :].rearrange("p (a b) -> p a b", a=E), ALU.mult))
                        pool.tensor_tensor(r3, r3, e3, ALU.add).then_inc(sig["f1_rank"], 1)

                    def norm_of_x(g):
                        after(pool, "f0_sq", g)
                        pool.tensor_tensor(rstd[g][:, 1:2], rstd[g][:, 0:1], mhalf[:, :], ALU.pow).then_inc(sig["f0_rnorm"], 1)

                    for stage in STAGES:
                        l, s = stage.split("_")
                        for g in range(G):
                            if l in ("a0", "a1", "a2") and s == "B":
                                masks(l, g)
                                if l != "a1":
                                    bias_residual(l, g)
                            elif stage == "g0_B":
                                bias_residual("g0", g)
                            elif stage == "g0_C":
                                sampling_index(g)
                            elif stage == "f0_A":
                                norm_of_x(g)
                            elif (l in ("a0", "a1", "a2") and s == "G") or stage in ("g0_H", "f0_E"):
                                norms(l, g)
                            elif stage == "f1_B":
                                ranks_of(g)
                    for g in range(G):
                        rsqrt("f1", g, EPS_LN)
            nc.all_engine_barrier(sems_to_clear=turn_sems)
        nc.sync.wait_ge(out_stored, 16 * TILES + 1)
        nc.sync.wait_ge(tiles_loaded, 16 * 3 * G * (TURNS + 1))


def _layout(i):
    import numpy as np

    f = np.float32
    c = np.ascontiguousarray
    p = np.arange(P)
    a = {"x": i["x"], "ctx": i["ctx_1024"]}
    used = i["L0_attn_dist_emb"][S:S + WIN]
    a["rel_fwd"] = c(np.tile(used.T, (H16, 1)))
    a["rel_rev"] = c(np.tile(used[::-1].T, (H16, 1)))

    def split_heads(w, heads, d):
        return w.reshape(-1, heads // 2, 2, d).transpose(0, 2, 1, 3).reshape(w.shape[0], heads * d)

    def col(v):
        return c(v.reshape(-1, P).T)

    a["a0_wq"], a["a0_wk"] = i["L0_attn_Wq"], i["L0_attn_Wk"]
    a["a0_wv"] = c(split_heads(i["L0_attn_Wv"], H16, D8))
    a["a0_wo"] = i["L0_attn_Wo"]
    a["a0_bq"], a["a0_bk"] = col(i["L0_attn_bq"]), col(i["L0_attn_bk"])
    a["bc_a0_bv"] = c(split_heads(i["L0_attn_bv"][None], H16, D8).reshape(2, S))
    a["bc_a0_bo"] = i["L0_attn_bo"][None]
    a["bc_a0_gamma"], a["bc_a0_beta"] = i["L0_attn_ln_gamma"][None], i["L0_attn_ln_beta"][None]

    a["g0_wq"] = c(i["L0_xattn_Wq"].T)
    a["g0_bq"], a["bc_g0_bq"] = col(i["L0_xattn_bq"]), i["L0_xattn_bq"][None]
    wk = split_heads(i["L0_xattn_Wk"].T, H16, D8).reshape(D, 2, HP, 1, D8)
    wv = split_heads(i["L0_xattn_Wv"].T, H16, D8).reshape(D, 2, HP, 1, D8)
    a["g0_wkv"] = c(np.concatenate([wk, wv], 3).reshape(D, 2 * P))
    bk = split_heads(i["L0_xattn_bk"][None], H16, D8).reshape(2, 1, HP, 1, 1, D8)
    bv = split_heads(i["L0_xattn_bv"][None], H16, D8).reshape(2, 1, HP, 1, 1, D8)
    a["bc_g0_bkv"] = c(np.broadcast_to(np.concatenate([bk, bv], 4), (2, 2, HP, 2, 2, D8)).reshape(2, UNITS))
    order = np.arange(H16 * NK).reshape(HP, 2, NK).transpose(0, 2, 1).reshape(-1)
    a["g0_woff"] = c(i["L0_xattn_Woff"][order].T)
    a["bc_off"] = c(i["L0_xattn_boff"][order][None])
    a["bc_ref"] = c(np.broadcast_to((np.arange(NK) - 3).astype(f)[None, :, None], (HP, NK, 2)).reshape(1, NS))
    a["g0_wo"] = c(i["L0_xattn_Wo"].T)
    a["bc_g0_bo"] = i["L0_xattn_bo"][None]
    a["mask_bs"] = i["mask_BxS2_if0"]
    a["query_pos"] = (p % S).astype(f)[:, None]
    a["seq_of_tile"] = c((p[:, None, None] == 2 * np.arange(TILES)[None, None] + np.arange(2)[None, :, None])
                         .reshape(P, 2 * TILES).astype(f))
    a["ones64"] = np.ones((P, S), f)
    spread_rows = np.zeros((81, 4, NK, 2, S), np.float16)
    j = np.arange(S) - 32
    for n in range(4):
        for k in range(NK):
            for h in range(2):
                r = (n * NK + k) * 2 + h
                spread_rows[r, n, k, h] = 2 * j
                spread_rows[40 + r, n, k, h] = -1
    spread_rows[80] = 1 - j * j
    a["spread"] = spread_rows.reshape(81, 20 * P)

    a["centroids"] = i["L0_ffn_centroids"]
    a["w_routeT"] = c(i["L0_ffn_w_route"].T)
    a["f0_w1"] = c(i["L0_ffn_w1"].transpose(1, 0, 2).reshape(D, 512))
    a["f0_b1"] = c(i["L0_ffn_b1"].reshape(4, P).T)
    a["f0_w2"] = c(i["L0_ffn_w2"].reshape(4, P, D).transpose(1, 0, 2).reshape(P, 512))
    a["f0_b2"] = i["L0_ffn_b2"]
    a["expert_rows"] = c((np.arange(E)[:, None, None] == 2 * np.arange(4)[None, :, None] + (p // 64)[None, None])
                         .reshape(E, 4 * P).astype(f))

    def split_wide(w):
        return w.reshape(w.shape[0], H8 // 2, 2, D32).transpose(0, 2, 1, 3).reshape(w.shape[0], H8 * D32)

    a["a1_wq"] = c(i["L1_attn_Wq"].T)
    a["a1_wkv"] = c(i["L1_attn_Wkv_down"].T)
    a["a1_wk"] = c(i["L1_attn_Wk_up"].T)
    a["a1_wv"] = c(split_wide(i["L1_attn_Wv_up"].T))
    a["a1_wo"] = c(i["L1_attn_Wo"].T.reshape(2, P, D).transpose(1, 0, 2).reshape(P, 2 * D))

    a["a2_wq"], a["a2_wk"] = c(i["L1_xattn_Wq"].T), c(i["L1_xattn_Wk"].T)
    a["a2_wv"] = c(split_heads(i["L1_xattn_Wv"].T, H16, D8))
    a["a2_wo"] = c(i["L1_xattn_Wo"].T)
    a["a2_bq"], a["a2_bk"] = col(i["L1_xattn_bq"]), col(i["L1_xattn_bk"])
    a["bc_a2_bv"] = c(split_heads(i["L1_xattn_bv"][None], H16, D8).reshape(2, S))
    a["bc_a2_bo"] = i["L1_xattn_bo"][None]
    a["mask_ss"] = c(i["mask_1x1xSxS2_if1"].reshape(S, S))

    a["f1_gw"] = i["L1_ffn_gate_W"]
    a["bc_f1_gb"] = i["L1_ffn_gate_b"][None]
    a["f1_w"] = c(i["L1_ffn_expert_W"].transpose(1, 0, 2).reshape(D, E * D))
    a["f1_b"] = i["L1_ffn_expert_b"].reshape(1, E * D)
    a["ones_row"] = np.ones((1, P), f)
    e = np.arange(E)
    a["bc_lower"] = (e[None, :] < e[:, None]).reshape(1, E * E).astype(f)

    a["ident"] = np.eye(P, dtype=f)
    a["head16"] = (p[:, None] // D8 == np.arange(H16)[None]).astype(f)
    a["within4"] = (p[:, None] // D8 % 4 == np.arange(4)[None]).astype(f)
    a["group4"] = (p[:, None] // 32 == np.arange(4)[None]).astype(f)
    return {k: c(v) for k, v in a.items()}


def kernel(**inputs):
    import numpy as _np
    import concourse.bacc as _bacc
    from concourse import mybir as _mybir
    from concourse.bass_utils import run_bass_kernel_spmd as _run

    nc = _bacc.Bacc("TRN2", target_bir_lowering=False, num_devices=1)
    arrays, args = {}, {}
    for name, a in _layout({k: _np.asarray(v) for k, v in inputs.items()}).items():
        arrays[f"in_{name}"] = a
        args[name] = nc.dram_tensor(f"in_{name}", a.shape, _mybir.dt.from_np(a.dtype), kind="ExternalInput").ap()
    out = nc.dram_tensor("out_0", (B, S, D), _mybir.dt.float32, kind="ExternalOutput").ap()
    decoder_kernel(nc, args, out)
    r = _run(nc, [arrays], core_ids=[0])
    return r.results[0]["out_0"]
```

```python
from contextlib import ExitStack

import concourse.bass as bass
from concourse import mybir

F32 = mybir.dt.float32
F16 = mybir.dt.float16
BF16 = mybir.dt.bfloat16
I32 = mybir.dt.int32
ALU = mybir.AluOpType
ACT = mybir.ActivationFunctionType
AX = mybir.AxisListType.X

B, S, D = 128, 64, 128
P = 128
TILES = B * S // P
G = 2
PHASE = {"a0": 0, "g0": 1, "f0": 2, "a1": 2, "a2": 3, "f1": 3}
PHASES = 4
PAIRS = TILES // G
H16, D8 = 16, 8
H8, D32 = 8, 32
NK = 5
HP = H16 // 2
NS = HP * NK * 2
LAT = 64
E = 8
WIN = 2 * S - 1
R8 = float(D8) ** -0.5
R32 = float(D32) ** -0.5
NEG = -1e9 * float(D8) ** 0.5
EPS_LN = 1e-5
QT = 8
M_SLOTS = 4
UNITS = 512


SIGNALS = {}
for _l in ("a0", "a1", "a2"):
    SIGNALS.update({f"{_l}_{_n}": 1 for _n in ("xT", "shifted", "probs", "probsT0", "ctx", "ctxT", "added", "x")})
    SIGNALS.update({f"{_l}_qk": 2 if _l == "a1" else 5, f"{_l}_masked": 2 if _l == "a1" else 1, f"{_l}_v": 2})
for _n in ("a0_probsT1", "a2_probsT1", "a0_xb", "a2_xb", "a0_summed", "a2_where", "a2_cT", "a1_latent",
           "g0_xT", "g0_cT", "g0_qT", "g0_qtok", "g0_xb", "g0_kv", "g0_hi", "g0_rest", "g0_mid", "g0_lo", "g0_pos", "g0_dist",
           "g0_idxT", "g0_hat", "g0_products", "g0_shifted", "g0_probs", "g0_weights", "g0_weighted", "g0_ctx", "g0_ctxT",
           "g0_added", "g0_x",
           "f0_xT", "f0_sq", "f0_rnorm", "f0_logits", "f0_shifted", "f0_exp", "f0_gates", "f0_gatesT", "f0_gated", "f0_added",
           "f0_x",
           "f1_xT", "f1_scored", "f1_shifted", "f1_exp", "f1_p", "f1_rank", "f1_gates", "f1_gatesT", "f1_mixed", "f1_biased",
           "out_x"):
    SIGNALS[_n] = 1
SIGNALS.update({"g0_idx": 2, "g0_onehot": 10, "g0_sampled": 8, "f0_h": 4})
for _n in ("a0i", "a0", "g0", "f0", "a1", "a2", "f1"):
    SIGNALS.update({f"{_n}_var": 1, f"{_n}_rstd": 1})


def order_of(phases):
    return [(stage, g) for stage, g in ORDER if g // G in phases]


def psum_plan(order):
    plan = {"M": {}, "S": {}}
    for stage, g in order:
        for kind, name in STAGE_USES.get(stage, ()):
            d = plan[kind]
            n = M_SLOTS if kind == "M" else 2
            before = list(d)[len(d) - n] if len(d) >= n else None
            d[(name, g)] = (len(d) % n, len(d) // n, before)
    return plan


def slots(stage):
    p = PHASE[stage[:2]]
    return range(p * G, (p + 1) * G)


ORDER = [(item[:-2], int(item[-1])) for item in """
    a0_A.0 f0_A.4 a0_A.1 a2_A.6 g0_A.2 g0_A.3 a2_A.7 a0_B.0 f0_A.5 a2_V.6 a0_B.1 a0_V.0 a2_B.6 a2_B.7 f0_B.4 a0_C.0
    g0_B.2 f0_B.5 a2_C.6 g0_B.3 g0_C.2 a2_C.7 a0_D.0 g0_C.3 a0_C.1 a0_V.1 a0_E.0 a2_D.6 a2_V.7 a0_D.1 f0_C.4 a2_D.7
    f0_C.5 g0_B2.2 g0_B2.3 f0_D.4 a0_F.0 g0_B3.2 g0_B3.3 f0_D.5 a0_E.1 g0_D.2 f0_E.4 f0_F.4 a2_E.6 a0_F.1 f0_E.5
    a2_F.6 a1_A.4 g0_E0.2 f0_F.5 a2_E.7 a1_L.4 a0_G.0 a2_F.7 a1_A.5 a2_G.6 g0_D.3 a2_G.7 a2_H.6 a1_B.4 g0_E0.3 a1_V.4
    a2_H.7 a0_G.1 f1_A.6 a1_C.4 f1_B.6 f1_A.7 g0_F0.2 f1_B2.6 a0_H.0 f1_B.7 a1_L.5 a0_H.1 g0_F0.3 g0_E1.2 f1_B2.7
    f1_C.6 a0_I.0 a1_B.5 g0_F1.2 f1_D.6 g0_E1.3 f1_C.7 a1_D.4 g0_F1.3 f1_E.6 g0_G.2 a1_C.5 g0_G.3 a1_E.4 g0_G2.2
    a1_D.5 g0_G2.3 a1_F.4 a1_V.5 a1_G.4 f1_D.7 a1_E.5 g0_G3.2 a1_F.5 g0_G3.3 f1_E.7 a1_H.4 g0_H.2 g0_H.3 a1_G.5 a0_I.1
    g0_I.2 g0_I.3 a1_H.5
""".split()]
STAGE_USES = {}
for _l in ("a0", "a1", "a2"):
    STAGE_USES.update({
        f"{_l}_A": [("M", f"{_l}_xT")],
        f"{_l}_B": [("M", f"{_l}_qk")],
        f"{_l}_V": [("M", f"{_l}_v")],
        f"{_l}_C": [("S", f"{_l}_scores")],
        f"{_l}_D": [("M", f"{_l}_pT0")] + ([("M", f"{_l}_pT1")] if _l != "a1" else []),
        f"{_l}_E": [("M", f"{_l}_pv")],
        f"{_l}_F": [("M", f"{_l}_cT")],
        f"{_l}_G": [("M", f"{_l}_o")],
    })
STAGE_USES["a1_L"] = [("M", "a1_lat")]
STAGE_USES.update({
    "g0_A": [("M", "g0_xT")],
    "g0_B": [("M", "g0_q"), ("M", "g0_kv")],
    "g0_C": [("M", "g0_off")],
    "g0_D": [("M", "g0_idxT")],
    "g0_E0": [("M", f"g0_eq{n}") for n in range(5)],
    "g0_F0": [("M", f"g0_s{n}") for n in range(HP // 2)],
    "g0_E1": [("M", f"g0_eq{n}") for n in range(5, 10)],
    "g0_F1": [("M", f"g0_s{n}") for n in range(HP // 2, HP)],
    "g0_G3": [("M", "g0_cT")],
    "g0_H": [("M", "g0_o")],
    "f0_A": [("M", "f0_xT")],
    "f0_B": [("M", "f0_lg"), ("M", "f0_h")],
    "f0_C": [("M", "f0_gT")],
    "f0_D": [("M", "f0_gb")],
    "f0_E": [("M", "f0_o")],
    "f1_A": [("M", "f1_xT")],
    "f1_B": [("M", "f1_gs")],
    "f1_C": [("S", "f1_y"), ("M", "f1_gT")],
    "f1_D": [("M", "f1_b")],
})


READ_BY = {"a0_scores": "a0_summed", "a1_scores": "a1_shifted", "a2_scores": "a2_shifted", "a1_lat": "a1_latent",
           "g0_xT": "g0_cT", "g0_q": "g0_qtok", "g0_kv": "g0_kv", "g0_off": "g0_pos", "g0_idxT": "g0_idxT",
           "f0_xT": "f0_xT", "f0_lg": "f0_logits", "f0_h": "f0_h", "f0_gT": "f0_gatesT", "f0_gb": "f0_gated",
           "f1_xT": "f1_xT", "f1_gs": "f1_scored", "f1_y": "f1_mixed", "f1_gT": "f1_gatesT", "f1_b": "f1_biased", "a0_xT": "a0_xT", "a1_xT": "a1_xT", "a2_xT": "a2_cT"}
for _l in ("a0", "a1", "a2"):
    READ_BY.update({f"{_l}_qk": f"{_l}_qk", f"{_l}_v": f"{_l}_v", f"{_l}_pT0": f"{_l}_probsT0", f"{_l}_pT1": f"{_l}_probsT1",
                    f"{_l}_pv": f"{_l}_ctx"})
for _l in ("a0", "g0", "f0", "a1", "a2"):
    READ_BY.update({f"{_l}_cT": f"{_l}_ctxT", f"{_l}_o": f"{_l}_added"})
IN_FIRST_HALF = {"g0_sampled": 4, "g0_onehot": 5}
for _n in range(10):
    READ_BY[f"g0_eq{_n}"] = ("g0_onehot", _n + 1)
for _n in range(HP):
    READ_BY[f"g0_s{_n}"] = ("g0_sampled", _n + 1)


def spread(ap, axis, n):
    u = ap.unsqueeze(axis)
    shape = list(u.shape)
    shape[axis] = n
    return u.broadcast_to(shape)


def decoder_kernel(nc, A, out):
    tok = lambda a: a.rearrange("b s d -> (b s) d").rearrange("(t p) d -> t p d", p=P)
    x_t, ctx_t, out_t = tok(A["x"]), tok(A["ctx"]), tok(out)
    rel = nc.dram_tensor("rel_scores", [B, S, H16, S], F32, kind="Internal").ap()
    rel_t = rel.rearrange("b l h r -> (b l) (h r)").rearrange("(t p) n -> t p n", p=P)

    with ExitStack() as ctx:
        def sb(name, shape, dt=F32, c=ctx):
            return c.enter_context(nc.sbuf_tensor(name, shape, dt))

        def sem(name):
            return ctx.enter_context(nc.semaphore(name))

        psS = ctx.enter_context(nc.psum_tensor("psS", [P, 2, 2 * UNITS], F32))
        psM = ctx.enter_context(nc.psum_tensor("psM", [P, M_SLOTS, UNITS], F32))

        loaded_weights = sem("loaded_weights")
        prepared = sem("prepared")
        x8_loaded = sem("x8_loaded")
        rel_stored = sem("rel_stored")
        x_loaded = sem("x_loaded")
        c_loaded = {p: sem(f"c_loaded{p}") for p in (1, 3)}
        out_stored = sem("out_stored")
        sig = {n: sem(n) for n in SIGNALS}
        m_full = [sem(f"m_full{i}") for i in range(M_SLOTS)]
        s_full = [sem(f"s_full{i}") for i in range(2)]
        dve_step = sem("dve_step")
        table_filled = {g: sem(f"table_filled{g}") for g in slots("g0")}
        rel_loaded = [sem(f"rel_loaded{g}") for g in range(G)]
        k_full, q_full, k_free, q_free, pair_ready = (sem(f"rel_{n}") for n in ("k_full", "q_full", "k_free", "q_free", "pair_ready"))
        pool_step = sem("pool_step")
        turn_sems = range(sig[next(iter(SIGNALS))].num, pool_step.num + 1)

        W = {}
        for name, a in A.items():
            if name in ("x", "ctx") or name.startswith("rel_") or name.startswith("bc_"):
                continue
            W[name] = sb("w_" + name, list(a.shape), a.dtype)
        for name, a in A.items():
            if name.startswith("bc_"):
                W[name] = sb("w_" + name, [P, a.shape[-1]])
        c_normT = sb("c_normT", [P, 2 * E])
        lens = sb("lens", [P, 3, TILES])
        masked = sb("masked", [P, S], I32)
        negs = sb("negs", [P, 1])
        mhalf = sb("mhalf", [P, 1])
        bqm = {l: sb(f"{l}_bqm", [P, 4]) for l in ("a0", "a2")}
        emb = sb("emb", [P, 2, WIN])
        n_loads = 2 + len(W) + sum(1 for n in W if n.startswith("bc_") and A[n].shape[0] == 2) + 1
        ident = W["ident"]

        c1 = ExitStack()
        x8 = sb("x8", [P, QT, D], c=c1)

        with ExitStack() as c0:
            cn = sb("cn", [E, P], c=c0)
            cn2 = sb("cn2", [E, P], c=c0)
            css = sb("css", [E, 4], c=c0)
            lrow = sb("lrow", [P, 2], c=c0)
            maskf = sb("maskf", [P, S], c=c0)
            lsel = sb("lsel", [P, 2, TILES], c=c0)
            m2 = sb("m2", [P, S], I32, c=c0)
            with nc.Block() as block:
                @block.sync
                def _(sp):
                    sp.sem_inc(rel_stored, 1)
                    sp.sem_inc(out_stored, 1)
                    sp.dma_start(x8[:, :, :], x_t[0:QT].rearrange("g p d -> p g d")).then_inc(x8_loaded, 16)
                    for name, w in W.items():
                        a = A[name]
                        if name.startswith("bc_"):
                            rows = a.shape[0]
                            for i in range(rows):
                                n = P // rows
                                sp.dma_start(w[i * n:(i + 1) * n, :],
                                             a[i:i + 1, :].broadcast_to([n, a.shape[1]])).then_inc(loaded_weights, 16)
                        else:
                            sp.dma_start(w[:], a).then_inc(loaded_weights, 16)
                    sp.dma_start(emb[:, 0, :], A["rel_fwd"]).then_inc(loaded_weights, 16)
                    sp.dma_start(emb[:, 1, :], A["rel_rev"]).then_inc(loaded_weights, 16)
                    sp.dma_start(m2[S:P, :], A["mask_ss"]).then_inc(loaded_weights, 16)

                @block.vector
                def _(dve):
                    steps = [0]

                    def link(ins):
                        steps[0] += 1
                        ins.then_inc(dve_step, 1)
                        dve.wait_ge(dve_step, steps[0])

                    dve.wait_ge(loaded_weights, 16 * n_loads)
                    link(dve.memset(mhalf[:, :], -0.5))
                    link(dve.tensor_tensor(W["bc_off"][:, :], W["bc_off"][:, :], W["bc_ref"][:, :], ALU.add))
                    for l in ("a0", "a2"):
                        link(dve.tensor_scalar(bqm[l][:, :], W["group4"][:, :], W[f"{l}_bq"][:, 0:1], None, ALU.mult))
                    link(dve.tensor_copy(m2[0:S, :], W["mask_ss"][:, :]))
                    link(dve.tensor_scalar(masked[:, :], m2[:, :], 0.0, None, ALU.is_equal))
                    link(dve.memset(negs[:, :], NEG))
                    link(dve.tensor_scalar(maskf[:, :], W["mask_bs"][:, :], -1.0, 1.0, ALU.mult, ALU.add))
                    link(dve.tensor_reduce(lrow[:, 0:1], maskf[:, :], AX, ALU.add))
                    link(dve.tensor_scalar(lrow[:, 1:2], lrow[:, 0:1], -1.0, None, ALU.add))
                    for p in range(2):
                        dve.tensor_scalar(lsel[:, p, :], W["seq_of_tile"][:, p * TILES:(p + 1) * TILES], lrow[:, 1:2],
                                          None, ALU.mult).then_inc(prepared, 1)
                    link(dve.tensor_tensor(cn2[:, :], W["centroids"][:, :], W["centroids"][:, :], ALU.mult))
                    dve.tensor_reduce(css[:, 0:1], cn2[:, :], AX, ALU.add).then_inc(prepared, 1)
                    dve.wait_ge(m_full[0], 1)
                    link(dve.tensor_copy(lens[:, 0, :], psM[:, 0, 0:TILES]))
                    link(dve.reciprocal(lens[:, 1, :], lens[:, 0, :]))
                    link(dve.tensor_scalar(lens[:, 2, :], lens[:, 0, :], 0.0, None, ALU.max))
                    dve.wait_ge(pool_step, 1)
                    link(dve.tensor_scalar(css[:, 2:3], css[:, 1:2], 1e12, None, ALU.min))
                    dve.tensor_scalar(cn[:, :], W["centroids"][:, :], css[:, 2:3], None, ALU.mult).then_inc(prepared, 1)
                    dve.wait_ge(m_full[1], 1)
                    link(dve.tensor_copy(c_normT[:, 0:E], psM[:, 1, 0:E]))
                    link(dve.tensor_copy(c_normT[:, E:2 * E], W["w_routeT"][:, :]))

                @block.gpsimd
                def _(pool):
                    pool.wait_ge(prepared, 3)
                    pool.wait_ge(dve_step, 1)
                    pool.tensor_tensor(css[:, 1:2], css[:, 0:1], mhalf[0:E, :], ALU.pow).then_inc(pool_step, 1)

                @block.tensor
                def _(pe):
                    pe.wait_ge(prepared, 2)
                    pe.wait_ge(loaded_weights, 16 * n_loads)
                    for p in range(2):
                        mm = pe.matmul(psM[S * p:S * p + S, 0, 0:TILES], W["ones64"][:, :], lsel[:, p, :],
                                       start=True, stop=True)
                    mm.then_inc(m_full[0], 1)
                    pe.wait_ge(prepared, 4)
                    pe.transpose(psM[:, 1, 0:E], cn[:, :], ident[0:E, 0:E]).then_inc(m_full[1], 1)
            nc.all_engine_barrier(sems_to_clear=turn_sems)

        with c1:
            q_all = sb("q_all", [P, B * S], c=c1)
            k_all = sb("k_all", [P, B * S], c=c1)
            with ExitStack() as c2:
                xT_half = sb("xT_half", [P, 2, UNITS], c=c2)
                with nc.Fori(0, TILES // QT) as it:
                    with nc.Block() as block:
                        q_done, k_done = (m_full[2], s_full[0]), (m_full[3], s_full[1])
                        q_ps, k_ps = (psM[:, 2, :], psS[:, 0, 0:UNITS]), (psM[:, 3, :], psS[:, 1, 0:UNITS])

                        @block.sync
                        def _(sp):
                            sp.wait_ge(m_full[1], 1)
                            sp.dma_start(x8[:, :, :], x_t[bass.ds((it + 1) % (TILES // QT) * QT, QT)].rearrange(
                                "g p d -> p g d")).then_inc(x8_loaded, 16)

                        @block.tensor
                        def _(pe):
                            pe.wait_ge(x8_loaded, it * 16 + 16)
                            for h in range(2):
                                for g in range(4):
                                    mm = pe.transpose(psM[:, h, g * P:(g + 1) * P],
                                                      x8[:, 4 * h + g, :], ident[:, :])
                                mm.then_inc(m_full[h], 1)
                            for h in range(2):
                                pe.wait_ge(sig["a0_xT"], h + 1)
                                for w, ps, full in (("a0_wk", k_ps, k_done), ("a0_wq", q_ps, q_done)):
                                    pe.matmul(ps[h], W[w][:, :], xT_half[:, h, :], start=True, stop=True).then_inc(full[h], 1)

                        @block.scalar
                        def _(act):
                            for h in range(2):
                                act.wait_ge(m_full[h], 1)
                                act.copy(xT_half[:, h, :], psM[:, h, :]).then_inc(sig["a0_xT"], 1)
                            for h in range(2):
                                act.wait_ge(q_done[h], 1)
                                act.activation(q_all[:, bass.ds(it * (2 * UNITS) + h * UNITS, UNITS)], q_ps[h], ACT.Identity,
                                               bias=W["a0_bq"][:, 0:1])

                        @block.vector
                        def _(dve):
                            for h in range(2):
                                dve.wait_ge(k_done[h], 1)
                                dve.tensor_scalar(k_all[:, bass.ds(it * (2 * UNITS) + h * UNITS, UNITS)], k_ps[h],
                                                  W["a0_bk"][:, 0:1], None, ALU.add)
                    nc.all_engine_barrier(sems_to_clear=turn_sems)

            with ExitStack() as c2:
                rbuf = [sb(f"rbuf{i}", [P, S, 2, S], c=c2) for i in range(2)]
                epair = sb("epair", [P, 2, 2, 2, WIN], c=c2)
                q_l = q_all[:, :].rearrange("p (b s) -> p s b", s=S)
                k_r = k_all[:, :].rearrange("p (b s) -> p s b", s=S)
                CH = 4
                NCH = S // CH
                banks = [psM[:, i, :] for i in range(M_SLOTS)] + [psS[:, i // 2, (i % 2) * UNITS:(i % 2 + 1) * UNITS] for i in range(4)]
                with nc.Fori(0, HP // 2) as it:
                    with nc.Block() as block:
                        @block.tensor
                        def _(pe):
                            for j in range(2):
                                pe.wait_ge(pair_ready, 4 * (j + 1))
                                for c in range(NCH):
                                    n = j * NCH + c
                                    if n >= 4:
                                        pe.wait_ge(k_free, n - 3)
                                    for i in range(CH):
                                        r = c * CH + i
                                        mm = pe.matmul(banks[n % 4][:, i * P:(i + 1) * P], k_r[:, r, :],
                                                       epair[:, j, 0, :, S - 1 - r:2 * S - 1 - r], start=True, stop=True)
                                    mm.then_inc(k_full, 1)
                                for c in range(NCH):
                                    n = j * NCH + c
                                    if n >= 4:
                                        pe.wait_ge(q_free, n - 3)
                                    for i in range(CH):
                                        l = c * CH + i
                                        mm = pe.matmul(banks[4 + n % 4][:, i * P:(i + 1) * P], q_l[:, l, :],
                                                       epair[:, j, 1, :, S - 1 - l:2 * S - 1 - l], start=True, stop=True)
                                    mm.then_inc(q_full, 1)

                        @block.scalar
                        def _(act):
                            act.wait_ge(rel_stored, it * (16 * NCH) + 1)
                            for j in range(2):
                                for c in range(NCH):
                                    n = j * NCH + c
                                    act.wait_ge(k_full, n + 1)
                                    src = banks[n % 4].rearrange("p (r h l) -> p r h l", h=2, l=S)
                                    for h in range(2):
                                        ins = act.copy(rbuf[j][:, :, h, c * CH:(c + 1) * CH].rearrange("p l r -> p r l"), src[:, :, h, :])
                                    ins.then_inc(k_free, 1)

                        @block.vector
                        def _(dve):
                            for j in range(2):
                                for way in range(2):
                                    for h in range(2):
                                        dve.tensor_scalar(epair[:, j, way, h, :], emb[:, way, :],
                                                          W["head16"][:, bass.ds(it * 4 + (2 * j + h), 1)], None,
                                                          ALU.mult).then_inc(pair_ready, 1)
                            for j in range(2):
                                dve.wait_ge(k_free, (j + 1) * NCH)
                                for c in range(NCH):
                                    n = j * NCH + c
                                    dve.wait_ge(q_full, n + 1)
                                    part = rbuf[j][:, c * CH:(c + 1) * CH, :, :].rearrange("p l h r -> p (l h r)")
                                    dve.tensor_tensor(part, banks[4 + n % 4], part, ALU.add).then_inc(q_free, 1)

                        @block.sync
                        def _(sp):
                            for j in range(2):
                                for c in range(NCH // 2):
                                    sp.wait_ge(q_free, j * NCH + 2 * c + 2)
                                    sp.dma_start(
                                        rel[:, 2 * c * CH:2 * (c + 1) * CH, bass.ds((it * 2 + j) * 2, 2), :],
                                        rbuf[j][:, 2 * c * CH:2 * (c + 1) * CH, :, :]).then_inc(rel_stored, 16)
                    nc.all_engine_barrier(sems_to_clear=turn_sems)

        def gs(name, shape, phases, dt=F32):
            return [sb(f"{name}{g}", shape, dt) if g // G in phases else None for g in range(PHASES * G)]

        def view(buffers, phases, f):
            return [f(buffers[g]) if g // G in phases else None for g in range(PHASES * G)]

        x_in = gs("x_in", [P, D], (0,))
        c_in = gs("c_in", [P, D], (1, 3))
        x_g = gs("x_g", [P, D], (1,))
        x_f = gs("x_f", [P, D], (2,))
        x_l = gs("x_l", [P, D], (2,))
        x_c = gs("x_c", [P, D], (3,))
        x_m = gs("x_m", [P, D], (3,))
        x_out = gs("x_out", [P, D], (3,))
        xT = gs("xT", [P, P], (0, 1, 2, 3))
        cT = gs("cT", [P, P + 1], (1, 3))
        xb = gs("xb", [P, D], (0, 1, 3))
        rmax = gs("rmax", [P, H16], (0, 1, 2, 3))
        hbuf = gs("hbuf", [P, D], (0, 1, 2, 3))
        stat = gs("stat", [P, 6], (0, 1, 2, 3))
        mv = gs("mv", [P, 2], (0, 1, 2, 3))
        rstd = gs("rstd", [P, 2], (0, 1, 2, 3))
        small = gs("small", [P, 3, NS], (1, 2, 3))
        latT = gs("latT", [LAT, P], (2, 3))
        v16 = gs("v16", [P, 2, HP, 2, D8 + 1], (0, 3))
        v32 = gs("v32", [P, 2, H8 // 2, 2, D32 + 1], (2,))
        mix = gs("mix", [P, 4 * P], (0, 1, 2, 3))
        att = view(mix, (0, 1, 2, 3), lambda w: w[:, 0:2 * P])
        attT = view(mix, (0, 1, 2, 3), lambda w: w[:, 2 * P:4 * P].rearrange("p (c q) -> p c q", c=2))
        probs = [sb(f"probs{g}", [P, 512 if g // G == 2 else 1024]) if g // G != 1 else None for g in range(PHASES * G)]
        work = gs("work", [P, 1024], (0, 2, 3))
        probsT = view(work, (0, 2, 3), lambda w: w[:, :].rearrange("p (n q) -> p n q", n=HP))
        qm = view(work, (0, 3), lambda w: w[:, 0:512].rearrange("p (c q) -> p c q", c=4))
        kbd = [None if g // G == 1 else work[g][:, 0:1024].rearrange("p (t b h r) -> p t b h r", t=2, b=2, h=4) if g // G == 2
               else work[g][:, 512:1024].rearrange("p (t b h r) -> p t b h r", t=1, b=2, h=4) for g in range(PHASES * G)]
        hT = view(work, (2,), lambda w: w[:, 512:1024])
        qk_sb = [sb(f"qk_sb{g}", [P, (2, 1, 4, 2)[g // G], P]) for g in range(PHASES * G)]
        pw = view(mix, (1, 3), lambda w: w[:, 0:4 * NS].rearrange("p (i n) -> p i n", i=4))
        ranks = view(mix, (3,), lambda w: w[:, 2 * NS:2 * NS + E * E])
        pos = view(mix, (1,), lambda w: w[:, 4 * NS:5 * NS])
        posi = view(mix, (1,), lambda w: w[:, 5 * NS:6 * NS].bitcast(I32))
        q_tok = hbuf
        dist = gs("dist", [P, 2, NS], (1,))
        hat = gs("hat", [P, HP * NK, 2, 2], (1,))
        idx = gs("idx", [P, 2, 81], (1,))
        idxT = gs("idxT", [81, 2, P], (1,), F16)
        low = gs("low", [P, 1280], (1,))
        onehot = view(low, (1,), lambda w: w[:, :].bitcast(BF16).rearrange("p (n q) -> p n q", q=P))
        kv = view(low, (1,), lambda w: w[:, 0:UNITS])
        kvc = view(low, (1,), lambda w: w[:, UNITS:1280].bitcast(BF16).rearrange("p (c n) -> p c n", c=3))
        bigp = view(low, (1,), lambda w: w[:, :])
        table = gs("table", [P, 3, 2, UNITS], (1,), BF16)
        wts = view(mix, (1,), lambda w: w[:, 2 * P:2 * P + 2 * NS])
        lc = gs("lc", [P, 3], (1,))
        samp = gs("samp", [P, 2 * HP * NK, 32], (1,))

        def after(eng, name, g, k=None):
            per = SIGNALS[name]
            k = per if k is None else k
            g = g % G
            first = IN_FIRST_HALF.get(name, per)
            eng.wait_ge(sig[name], g * first + k if k <= first else G * first + g * (per - first) + k - first)

        def await_reader(pe, use):
            name, g = use
            who = READ_BY[name]
            if isinstance(who, tuple):
                after(pe, who[0], g, who[1])
            else:
                after(pe, who, g)

        def fullM(eng, name, g):
            s, n, _ = plan["M"][(name, g)]
            eng.wait_ge(m_full[s], n + 1)
            return psM[:, s, :]

        def takeM(pe, name, g):
            s, _, before = plan["M"][(name, g)]
            if before:
                await_reader(pe, before)
            return psM[:, s, :], m_full[s]

        def fullS(eng, name, g):
            s, n, _ = plan["S"][(name, g)]
            eng.wait_ge(s_full[s], n + 1)
            return psS[:, s, :]

        def takeS(pe, name, g):
            s, _, before = plan["S"][(name, g)]
            if before:
                await_reader(pe, before)
            return psS[:, s, :], s_full[s]

        heads_of = {"a0": (H16, D8), "a1": (H8, D32), "a2": (H16, D8)}
        x_of = {"a0": x_in, "g0": x_g, "f0": x_f, "a1": x_l, "a2": x_c, "f1": x_m}
        next_of = {"a0": "g0", "g0": "f0", "f0": "a1", "a1": "a2", "a2": "f1"}
        x_ready = {"a1": "f0_x", "f1": "a2_x"}

        wo_of = {"a0": "a0_wo", "g0": "g0_wo", "a1": "a1_wo", "a2": "a2_wo"}

        def tile(pair, g):
            return bass.ds(pair * G + g % G, 1)

        all_rel = 16 * (S // 8) * HP + 1
        with nc.Block() as block:
            @block.vector
            def _(dve):
                dve.wait_ge(rel_stored, all_rel)
                n = 0
                for l, v, d in (("a0", v16, D8), ("a1", v32, D32), ("a2", v16, D8)):
                    for g in slots(l):
                        n += 1
                        dve.memset(v[g][:], 0.0).then_inc(dve_step, 1)
                        dve.wait_ge(dve_step, n)
                        for p in range(2):
                            dve.memset(v[g][S * p:S * p + S, :, :, p, d:d + 1], 1.0)
                for g in slots("g0"):
                    dve.memset(idx[g][:, :, 80:81], 1.0)
                    dve.memset(cT[g][:, P:P + 1], 0.0)

            @block.gpsimd
            def _(pool):
                pool.wait_ge(rel_stored, all_rel)
                for g in slots("g0"):
                    pool.memset(table[g][:], 0.0).then_inc(pool_step, 1)

            @block.sync
            def _(sp):
                sp.wait_ge(x8_loaded, 16 * (TILES // QT + 1))
                sp.wait_ge(rel_stored, all_rel)
                for g in slots("a0"):
                    sp.dma_start(x_in[g][:, :], x_t[g]).then_inc(x_loaded, 16)
                for l in ("g0", "a2"):
                    for g in slots(l):
                        sp.dma_start(c_in[g][:, :], ctx_t[g % G]).then_inc(c_loaded[PHASE[l]], 16)
        nc.all_engine_barrier(sems_to_clear=turn_sems)

        plan = {}

        def turn(it, phases):
            order = order_of(phases)
            plan.update(psum_plan(order))
            in_loop = not isinstance(it, int)

            def done(l):
                return it - PHASE[l]

            with nc.Block() as block:
                @block.sync
                def _(sp):
                    for g in slots("a0") if 0 in phases else ():
                        sp.dma_start(probs[g][:, :], rel_t[tile(done("a0"), g)].rearrange("o p d -> (o p) d")).then_inc(rel_loaded[g], 16)

                    def next_context(l, g):
                        if not in_loop and done(l) + 1 == PAIRS:
                            return
                        after(sp, f"{l}_cT", g)
                        sp.dma_start(c_in[g][:, :], ctx_t[tile(done(l) + 1, g)].rearrange("o p d -> (o p) d")).then_inc(
                            c_loaded[PHASE[l]], 16)

                    def next_input(g):
                        after(sp, "a0_x", g)
                        sp.dma_start(x_in[g][:, :], x_t[tile((it + 1) % PAIRS, g)].rearrange("o p d -> (o p) d")).then_inc(x_loaded, 16)

                    def fill_table(g):
                        after(sp, "g0_hi", g)
                        after(sp, "g0_mid", g)
                        after(sp, "g0_lo", g)
                        for p in range(2):
                            r = slice(S * p, S * p + S)
                            sp.dma_start(table[g][r, :, p, :], kvc[g][r, :, :]).then_inc(table_filled[g], 16)

                    def store(g):
                        after(sp, "out_x", g)
                        sp.dma_start(out_t[tile(done("f1"), g)].rearrange("o p d -> (o p) d"), x_out[g][:, :]).then_inc(
                            out_stored, 16)

                    run = {"g0_C": lambda g: next_context("g0", g), "a2_C": lambda g: next_context("a2", g),
                           "g0_B3": fill_table, "f1_E": store, "a0_I": next_input}
                    for stage, g in order:
                        if stage in run:
                            run[stage](g)

                @block.tensor
                def _(pe):
                    def transpose_x(l, g):
                        if l in x_ready:
                            after(pe, x_ready[l], g)
                        elif g % G == 0 and l == "a0":
                            pe.wait_ge(x_loaded, (done(l) + 1) * (16 * G))
                        elif g % G == 0 and l in ("g0", "a2"):
                            pe.wait_ge(c_loaded[PHASE[l]], (done(l) + 1) * (16 * G))
                        ps, full = takeM(pe, f"{l}_xT", g)
                        mm = pe.transpose(ps[:, 0:P], x_of[l][g][:, :], ident[:, :])
                        if l in ("g0", "a2"):
                            mm = pe.transpose(ps[:, P:2 * P], c_in[g][:, :], ident[:, :])
                        mm.then_inc(full, 1)

                    def qk(l, g):
                        after(pe, f"{l}_xT", g)
                        if l == "a2":
                            after(pe, "a2_cT", g)
                        ps, full = takeM(pe, f"{l}_qk", g)
                        if l == "a1":
                            after(pe, "a1_latent", g)
                            for c in range(2):
                                pe.matmul(ps[:, c * P:(c + 1) * P], W["a1_wq"][:, c * P:(c + 1) * P], xT[g][:, :],
                                          start=True, stop=True)
                                mm = pe.matmul(ps[:, (2 + c) * P:(3 + c) * P], W["a1_wk"][:, c * P:(c + 1) * P],
                                               latT[g][:, :], start=True, stop=True)
                        else:
                            kin = xT[g][:, :] if l == "a0" else cT[g][:, 0:P]
                            pe.matmul(ps[:, 0:P], W[f"{l}_wq"][:, :], xT[g][:, :], start=True, stop=True)
                            mm = pe.matmul(ps[:, P:2 * P], W[f"{l}_wk"][:, :], kin, start=True, stop=True)
                        mm.then_inc(full, 1)

                    def values(l, g):
                        vin, vw, vk = {"a0": (xT, W["a0_wv"], S), "a1": (latT, W["a1_wv"], 2 * S), "a2": (cT, W["a2_wv"], S)}[l]
                        after(pe, {"a0": "a0_xT", "a1": "a1_latent", "a2": "a2_cT"}[l], g)
                        vin = vin[g]
                        ps, full = takeM(pe, f"{l}_v", g)
                        for b in range(2):
                            for p in range(2):
                                mm = pe.matmul(ps[S * p:S * p + S, b * vk:(b + 1) * vk], vin[:, b * S:(b + 1) * S],
                                               vw[:, p * vk:(p + 1) * vk], start=True, stop=True)
                        mm.then_inc(full, 1)

                    def scores(l, g):
                        after(pe, f"{l}_masked", g)
                        ps, full = takeS(pe, f"{l}_scores", g)
                        for b in range(2):
                            for c in range(2 if l == "a1" else 4):
                                lhs = (qk_sb[g] if l == "a1" else qm[g])[:, c, b * S:(b + 1) * S]
                                rhs = kbd[g][:, c if l == "a1" else 0, b, :, :].rearrange("p h r -> p (h r)")
                                mm = pe.matmul(ps[b * S:(b + 1) * S, c * 256:(c + 1) * 256], lhs, rhs, start=True, stop=True)
                        mm.then_inc(full, 1)

                    def transpose_probs(l, g):
                        after(pe, f"{l}_probs", g)
                        for c in range(1 if l == "a1" else 2):
                            ps, full = takeM(pe, f"{l}_pT{c}", g)
                            for i in range(4):
                                n = 4 * c + i
                                mm = pe.transpose(ps[:, i * P:(i + 1) * P], probs[g][:, n * P:(n + 1) * P], ident[:, :])
                            mm.then_inc(full, 1)

                    def probs_values(l, g):
                        heads, d = heads_of[l]
                        after(pe, f"{l}_probsT0", g)
                        if l != "a1":
                            after(pe, f"{l}_probsT1", g)
                        after(pe, f"{l}_v", g)
                        ps, full = takeM(pe, f"{l}_pv", g)
                        v = v32[g] if l == "a1" else v16[g]
                        w = 2 * (d + 1)
                        for n in range(heads // 2):
                            for b in range(2):
                                mm = pe.matmul(ps[b * S:(b + 1) * S, n * w:(n + 1) * w],
                                               probsT[g][:, n, b * S:(b + 1) * S],
                                               v[:, b, n, :, :].rearrange("p h d -> p (h d)"), start=True, stop=True)
                        mm.then_inc(full, 1)

                    def transpose_ctx(l, g):
                        after(pe, f"{l}_ctx", g)
                        ps, full = takeM(pe, f"{l}_cT", g)
                        for c in range(2 if l == "a1" else 1):
                            mm = pe.transpose(ps[:, c * P:(c + 1) * P], att[g][:, c * P:(c + 1) * P], ident[:, :])
                        mm.then_inc(full, 1)

                    def project(l, g):
                        after(pe, f"{l}_ctxT", g)
                        ps, full = takeM(pe, f"{l}_o", g)
                        n = 2 if l == "a1" else 1
                        for c in range(n):
                            mm = pe.matmul(ps[:, 0:D], attT[g][:, c, :], W[wo_of[l]][:, c * D:(c + 1) * D],
                                           start=(c == 0), stop=(c == n - 1))
                        mm.then_inc(full, 1)

                    def latent(g):
                        after(pe, "a1_xT", g)
                        ps, full = takeM(pe, "a1_lat", g)
                        pe.matmul(ps[0:LAT, 0:P], W["a1_wkv"][:, :], xT[g][:, :], start=True, stop=True).then_inc(full, 1)

                    def sample_inputs(g):
                        after(pe, "g0_xT", g)
                        after(pe, "g0_cT", g)
                        ps, full = takeM(pe, "g0_q", g)
                        pe.matmul(ps[:, 0:P], W["g0_wq"][:, :], xT[g][:, :], start=True, stop=True)
                        pe.matmul(ps[:, P:2 * P], xT[g][:, :], W["g0_wq"][:, :], start=True, stop=True).then_inc(full, 1)
                        ps, full = takeM(pe, "g0_kv", g)
                        dst = ps.rearrange("p (b n e w) -> p b e n w", b=2, n=HP, e=2)
                        for b in range(2):
                            for e in range(2):
                                for p in range(2):
                                    mm = pe.matmul(dst[S * p:S * p + S, b, e, :, :], cT[g][:, b * S + e:(b + 1) * S + e],
                                                   W["g0_wkv"][:, p * P:(p + 1) * P], start=True, stop=True)
                        mm.then_inc(full, 1)

                    def offsets(g):
                        after(pe, "g0_qT", g)
                        ps, full = takeM(pe, "g0_off", g)
                        pe.matmul(ps[:, 0:NS], qk_sb[g][:, 0, :], W["g0_woff"][:, :], start=True, stop=True).then_inc(full, 1)

                    def transpose_idx(g):
                        after(pe, "g0_idx", g)
                        ps, full = takeM(pe, "g0_idxT", g)
                        for c in range(2):
                            mm = pe.transpose(ps[0:81, c * P:(c + 1) * P], idx[g][:, c, :], ident[:, :])
                        mm.then_inc(full, 1)

                    def spread_idx(g, hf):
                        after(pe, "g0_idxT", g)
                        for u in range(5 * hf, 5 * hf + 5):
                            ps, full = takeM(pe, f"g0_eq{u}", g)
                            for i in range(4):
                                half, n = divmod(4 * u + i, 20)
                                mm = pe.matmul(ps[:, i * P:(i + 1) * P], W["spread"][:, n * P:(n + 1) * P],
                                               idxT[g][:, half, :], start=True, stop=True)
                            mm.then_inc(full, 1)

                    def sample(g, hf):
                        pe.wait_ge(table_filled[g], 32)
                        after(pe, "g0_onehot", g, 5 * hf + 5)
                        for n in range(4 * hf, 4 * hf + 4):
                            ps, full = takeM(pe, f"g0_s{n}", g)
                            for b in range(2):
                                for k in range(NK):
                                    for part in range(3):
                                        rhs = table[g][:, part, :, (b * HP + n) * 32:(b * HP + n + 1) * 32].rearrange(
                                            "p h (w d) -> p w h d", d=D8)
                                        mm = pe.matmul(ps[b * S:(b + 1) * S, k * 64:(k + 1) * 64],
                                                       onehot[g][:, (n - 4 * hf) * NK + k, b * S:(b + 1) * S], rhs,
                                                       start=(part == 0), stop=(part == 2))
                            mm.then_inc(full, 1)

                    def router(g):
                        after(pe, "f0_xT", g)
                        ps, full = takeM(pe, "f0_lg", g)
                        pe.matmul(ps[:, 0:2 * E], xT[g][:, :], c_normT[:, :], start=True, stop=True).then_inc(full, 1)
                        ps, full = takeM(pe, "f0_h", g)
                        for c in range(4):
                            mm = pe.matmul(ps[:, c * P:(c + 1) * P], W["f0_w1"][:, c * P:(c + 1) * P], xT[g][:, :],
                                           start=True, stop=True)
                        mm.then_inc(full, 1)

                    def transpose_gates(g):
                        after(pe, "f0_gates", g)
                        ps, full = takeM(pe, "f0_gT", g)
                        pe.transpose(ps[0:E, 0:P], small[g][:, 0, 0:E], ident[:, :]).then_inc(full, 1)

                    def spread_gates(g):
                        after(pe, "f0_gatesT", g)
                        ps, full = takeM(pe, "f0_gb", g)
                        for c in range(4):
                            mm = pe.matmul(ps[:, c * P:(c + 1) * P], W["expert_rows"][:, c * P:(c + 1) * P],
                                           latT[g][0:E, :], start=True, stop=True)
                        mm.then_inc(full, 1)

                    def experts_out(g):
                        after(pe, "f0_gated", g)
                        ps, full = takeM(pe, "f0_o", g)
                        for c in range(4):
                            pe.matmul(ps[:, 0:D], hT[g][:, c * P:(c + 1) * P], W["f0_w2"][:, c * D:(c + 1) * D],
                                      start=(c == 0), stop=False)
                        pe.matmul(ps[:, 0:D], latT[g][0:E, :], W["f0_b2"][:, :], start=False, stop=True).then_inc(full, 1)

                    def scores1(g):
                        after(pe, "f1_xT", g)
                        ps, full = takeM(pe, "f1_gs", g)
                        pe.matmul(ps[:, 0:E], xT[g][:, :], W["f1_gw"][:, :], start=True, stop=True).then_inc(full, 1)

                    def expert_outputs(g):
                        ps, full = takeS(pe, "f1_y", g)
                        for c in range(2):
                            o = ps[:, c * UNITS:(c + 1) * UNITS]
                            mm = pe.matmul(o, xT[g][:, :], W["f1_w"][:, c * UNITS:(c + 1) * UNITS], start=True, stop=True)
                        mm.then_inc(full, 1)

                    def transpose_gates1(g):
                        after(pe, "f1_gates", g)
                        ps, full = takeM(pe, "f1_gT", g)
                        pe.transpose(ps[0:E, 0:P], small[g][:, 0, 0:E], ident[:, :]).then_inc(full, 1)

                    def expert_bias(g):
                        after(pe, "f1_gatesT", g)
                        ps, full = takeM(pe, "f1_b", g)
                        pe.matmul(ps[:, 0:D], latT[g][0:E, :], W["f1_b"][:, :], start=True, stop=True).then_inc(full, 1)

                    run = {"g0_B": sample_inputs, "g0_C": offsets, "g0_D": transpose_idx, 
                           "g0_E0": lambda g: spread_idx(g, 0), "g0_F0": lambda g: sample(g, 0),
                           "g0_E1": lambda g: spread_idx(g, 1), "g0_F1": lambda g: sample(g, 1),
                           "f0_B": router, "f0_C": transpose_gates, "f0_D": spread_gates, "f0_E": experts_out,
                           "a1_L": latent, "f1_B": scores1,
                           "f1_C": lambda g: (expert_outputs(g), transpose_gates1(g)), "f1_D": expert_bias}
                    for stage, g in order:
                        l, s = stage.split("_")
                        if stage in run:
                            run[stage](g)
                        elif s == "A":
                            transpose_x(l, g)
                        elif stage == "g0_G3":
                            transpose_ctx(l, g)
                        elif stage == "g0_H":
                            project(l, g)
                        elif stage in STAGE_USES:
                            {"B": qk, "V": values, "C": scores, "D": transpose_probs, "E": probs_values, "F": transpose_ctx,
                             "G": project}[s](l, g)

                @block.scalar
                def _(act):
                    def copy_xT(l, g):
                        ps = fullM(act, f"{l}_xT", g)
                        ins = act.copy(xT[g][:, :], ps[:, 0:P])
                        ins.then_inc(sig[f"{l}_xT"], 1)
                        if l in ("g0", "a2"):
                            act.copy(cT[g][:, 0:P], ps[:, P:2 * P]).then_inc(sig[f"{l}_cT"], 1)

                    def copy_qk(l, g):
                        ps = fullM(act, f"{l}_qk", g)
                        if l == "a1":
                            act.copy(qk_sb[g][:, 0:2, :].rearrange("p c q -> p (c q)"), ps[:, 0:2 * P]).then_inc(sig["a1_qk"], 1)
                            act.copy(qk_sb[g][:, 2:4, :].rearrange("p c q -> p (c q)"), ps[:, 2 * P:4 * P]).then_inc(sig["a1_qk"], 1)
                        else:
                            for c in range(4):
                                act.activation(qm[g][:, c, :], ps[:, 0:P], ACT.Identity, bias=bqm[l][:, c:c + 1],
                                               scale=W["group4"][:, c:c + 1]).then_inc(sig[f"{l}_qk"], 1)
                            act.activation(qk_sb[g][:, 1, :], ps[:, P:2 * P], ACT.Identity,
                                           bias=W[f"{l}_bk"][:, 0:1]).then_inc(sig[f"{l}_qk"], 1)

                    def exponential(l, g):
                        n = heads_of[l][0] * S
                        after(act, f"{l}_shifted", g)
                        act.activation(probs[g][:, 0:n], probs[g][:, 0:n], ACT.Exp,
                                       scale=R32 if l == "a1" else R8).then_inc(sig[f"{l}_probs"], 1)

                    def copy_probsT(l, g):
                        ps = fullM(act, f"{l}_pT0", g)
                        act.copy(probsT[g][:, 0:4, :].rearrange("p n q -> p (n q)"), ps).then_inc(sig[f"{l}_probsT0"], 1)
                        if l != "a1":
                            ps = fullM(act, f"{l}_pT1", g)
                            act.copy(probsT[g][:, 4:8, :].rearrange("p n q -> p (n q)"), ps).then_inc(sig[f"{l}_probsT1"], 1)

                    def copy_ctxT(l, g):
                        ps = fullM(act, f"{l}_cT", g)
                        n = 2 if l == "a1" else 1
                        act.copy(attT[g][:, 0:n, :].rearrange("p c q -> p (c q)"), ps[:, 0:n * P]).then_inc(sig[f"{l}_ctxT"], 1)

                    def latent(g):
                        ps = fullM(act, "a1_lat", g)
                        act.copy(latT[g][:, :], ps[0:LAT, 0:P]).then_inc(sig["a1_latent"], 1)

                    def high_parts(g):
                        after(act, "g0_kv", g)
                        act.copy(kvc[g][:, 0, :], kv[g][:, :]).then_inc(sig["g0_hi"], 1)

                    def middle_parts(g):
                        after(act, "g0_rest", g)
                        act.copy(kvc[g][:, 1, :], kv[g][:, :]).then_inc(sig["g0_mid"], 1)

                    def hats(g):
                        after(act, "g0_dist", g)
                        act.activation(dist[g][:, :, :], dist[g][:, :, :], ACT.Abs).then_inc(sig["g0_hat"], 1)

                    def idxT_copy(g):
                        ps = fullM(act, "g0_idxT", g)
                        act.copy(idxT[g][:, :, :].rearrange("p c q -> p (c q)"), ps[0:81, 0:2 * P]).then_inc(sig["g0_idxT"], 1)

                    def onehots(g, hf):
                        act.wait_ge(table_filled[g], 32)
                        for u in range(5 * hf, 5 * hf + 5):
                            ps = fullM(act, f"g0_eq{u}", g)
                            act.activation(onehot[g][:, 4 * u - 20 * hf:4 * u - 20 * hf + 4, :].rearrange("p n q -> p (n q)"), ps,
                                           ACT.Relu).then_inc(sig["g0_onehot"], 1)

                    def copy_samples(g, hf):
                        for n in range(4 * hf, 4 * hf + 4):
                            ps = fullM(act, f"g0_s{n}", g)
                            act.copy(samp[g][:, n * 10:(n + 1) * 10, :].rearrange("p n w -> p (n w)"), ps[:, 0:NK * 64]).then_inc(
                                sig["g0_sampled"], 1)

                    def sample_exp(g):
                        after(act, "g0_shifted", g)
                        act.activation(small[g][:, 1, :], small[g][:, 1, :], ACT.Exp, scale=0.5 * R8).then_inc(sig["g0_probs"], 1)

                    def logits(g):
                        ps = fullM(act, "f0_lg", g)
                        act.copy(small[g][:, 2, 0:2 * E], ps[:, 0:2 * E]).then_inc(sig["f0_logits"], 1)
                        ps = fullM(act, "f0_h", g)
                        for c in range(4):
                            act.activation(hT[g][:, c * P:(c + 1) * P], ps[:, c * P:(c + 1) * P], ACT.Gelu,
                                           bias=W["f0_b1"][:, c:c + 1]).then_inc(sig["f0_h"], 1)

                    def gate_exp(g):
                        after(act, "f0_shifted", g)
                        act.activation(small[g][:, 1, 0:E], small[g][:, 1, 0:E], ACT.Exp).then_inc(sig["f0_exp"], 1)

                    def gatesT(g):
                        ps = fullM(act, "f0_gT", g)
                        act.copy(latT[g][0:E, :], ps[0:E, 0:P]).then_inc(sig["f0_gatesT"], 1)

                    def gatesT1(g):
                        ps = fullM(act, "f1_gT", g)
                        act.copy(latT[g][0:E, :], ps[0:E, 0:P]).then_inc(sig["f1_gatesT"], 1)

                    def gate1_exp(g):
                        after(act, "f1_shifted", g)
                        act.activation(small[g][:, 1, 0:E], small[g][:, 1, 0:E], ACT.Exp).then_inc(sig["f1_exp"], 1)

                    run = {"g0_B": [high_parts], "g0_B2": [middle_parts], "g0_D": [idxT_copy, hats],
                           "g0_E0": [lambda g: onehots(g, 0)], "g0_F0": [lambda g: copy_samples(g, 0)],
                           "g0_E1": [lambda g: onehots(g, 1)], "g0_F1": [lambda g: copy_samples(g, 1)],
                           "g0_G": [sample_exp], "g0_G3": [lambda g: copy_ctxT("g0", g)],
                           "f0_B": [logits, gate_exp], "f0_C": [gatesT], "a1_L": [latent],
                           "f1_B": [gate1_exp], "f1_C": [gatesT1]}
                    for l in ("a0", "g0", "f0", "a1", "a2", "f1"):
                        run[f"{l}_A"] = [lambda g, l=l: copy_xT(l, g)]
                    for l in ("a0", "a1", "a2"):
                        for s, f in (("B", copy_qk), ("C", exponential), ("D", copy_probsT), ("F", copy_ctxT)):
                            run[f"{l}_{s}"] = [lambda g, l=l, f=f: f(l, g)]
                    for stage, g in order:
                        for f in run.get(stage, ()):
                            f(g)

                @block.vector
                def _(dve):
                    steps = [0]

                    def link(ins):
                        steps[0] += 1
                        ins.then_inc(dve_step, 1)
                        dve.wait_ge(dve_step, steps[0])

                    def bc(name, n=D):
                        return W["bc_" + name][:, 0:n]

                    def values(l, g):
                        heads, d = heads_of[l]
                        ps = fullM(dve, f"{l}_v", g)
                        v = v32[g] if l == "a1" else v16[g]
                        n = heads // 2
                        for p in range(2):
                            r = slice(S * p, S * p + S)
                            src = ps[r, 0:2 * n * d].rearrange("p (b n d) -> p b n d", b=2, n=n)
                            if l == "a1":
                                ins = dve.tensor_copy(v[r, :, :, p, 0:d], src)
                            else:
                                bias = spread(W[f"bc_{l}_bv"][r, :].rearrange("p (n d) -> p n d", n=n), 1, 2)
                                ins = dve.tensor_tensor(v[r, :, :, p, 0:d], src, bias, ALU.add)
                            ins.then_inc(sig[f"{l}_v"], 1)

                    def shift(l, g):
                        heads = heads_of[l][0]
                        n = heads * S
                        ps = fullS(dve, f"{l}_scores", g)
                        pr = probs[g][:, 0:n]
                        pr3 = pr.rearrange("p (h r) -> p h r", r=S)
                        src = ps[:, 0:n]
                        if l == "a0":
                            dve.wait_ge(rel_loaded[g], 16)
                            dve.tensor_tensor(pr, src, pr, ALU.add).then_inc(sig["a0_summed"], 1)
                            after(dve, "a0_summed", g)
                            src = pr
                        if l == "a2":
                            dve.copy_predicated(src.rearrange("p (h r) -> p h r", r=S), spread(masked[:, :], 1, heads),
                                                spread(negs[:, 0:1].broadcast_to([P, heads]), 2, S)).then_inc(sig["a2_where"], 1)
                            after(dve, "a2_where", g)
                        link(dve.tensor_reduce(rmax[g][:, 0:heads], src.rearrange("p (h r) -> p h r", r=S), AX, ALU.max))
                        dve.tensor_tensor(pr3, src.rearrange("p (h r) -> p h r", r=S),
                                          spread(rmax[g][:, 0:heads], 2, S),
                                          ALU.subtract).then_inc(sig[f"{l}_shifted"], 1)

                    def masks(l, g):
                        after(dve, f"{l}_qk", g)
                        for t in range(2 if l == "a1" else 1):
                            src = qk_sb[g][:, 2 + t if l == "a1" else 1, :].rearrange("p (b r) -> p b r", b=2)
                            m = W["group4"] if l == "a1" else W["within4"]
                            dve.tensor_tensor(kbd[g][:, t, :, :, :], spread(src, 2, 4),
                                              spread(spread(m[:, :], 1, 2), 3, S), ALU.mult).then_inc(sig[f"{l}_masked"], 1)

                    def normalise(l, g):
                        heads, d = heads_of[l]
                        ps = fullM(dve, f"{l}_pv", g)
                        o = ps[:, 0:heads * (d + 1)].rearrange("p (h d) -> p h d", h=heads)
                        link(dve.reciprocal(rmax[g][:, 0:heads].unsqueeze(2), o[:, :, d:d + 1]))
                        dve.tensor_tensor(att[g][:, 0:heads * d].rearrange("p (h d) -> p h d", h=heads), o[:, :, 0:d],
                                          spread(rmax[g][:, 0:heads], 2, d), ALU.mult).then_inc(sig[f"{l}_ctx"], 1)

                    def moments(name, g):
                        link(dve.bn_stats(stat[g][:, :], hbuf[g][:, :]))
                        dve.bn_aggr(mv[g][:, :], stat[g][:, :]).then_inc(sig[f"{name}_var"], 1)

                    def norm(name, g, dst):
                        after(dve, f"{name}_rstd", g)
                        return dve.tensor_scalar(dst, hbuf[g][:, :], mv[g][:, 0:1], rstd[g][:, 1:2], ALU.subtract, ALU.mult)

                    def residual(l, g):
                        ps = fullM(dve, f"{l}_o", g)
                        add = x_of[l][g][:, :] if l in ("a1", "f0") else xb[g][:, :]
                        if l in ("a0", "g0", "a2"):
                            after(dve, f"{l}_xb", g)
                        dve.tensor_tensor(hbuf[g][:, :], ps[:, 0:D], add, ALU.add).then_inc(sig[f"{l}_added"], 1)
                        after(dve, f"{l}_added", g)
                        moments("a0i" if l == "a0" else l, g)

                    def inner_norm(g):
                        link(norm("a0i", g, hbuf[g][:, :]))
                        link(dve.tensor_tensor(hbuf[g][:, :], hbuf[g][:, :], bc("a0_gamma"), ALU.mult))
                        link(dve.tensor_tensor(hbuf[g][:, :], hbuf[g][:, :], bc("a0_beta"), ALU.add))
                        link(dve.tensor_tensor(hbuf[g][:, :], hbuf[g][:, :], x_in[g][:, :], ALU.add))
                        moments("a0", g)

                    def hand_over(l, g):
                        nl = next_of[l]
                        ng = g if PHASE[nl] == PHASE[l] else g + G
                        if ng != g and ng // G in phases:
                            after(dve, f"{nl}_xT", ng)
                            after(dve, "f0_added" if nl == "f0" else f"{nl}_xb", ng)
                        norm(l, g, x_of[nl][ng][:, :]).then_inc(sig[f"{l}_x"], 1)

                    def sample_inputs(g):
                        ps = fullM(dve, "g0_q", g)
                        dve.tensor_scalar(qk_sb[g][:, 0, :], ps[:, 0:P], W["g0_bq"][:, 0:1], None, ALU.add).then_inc(sig["g0_qT"], 1)
                        dve.tensor_tensor(q_tok[g][:, :], ps[:, P:2 * P], bc("g0_bq"), ALU.add).then_inc(sig["g0_qtok"], 1)
                        ps = fullM(dve, "g0_kv", g)
                        dve.tensor_tensor(kv[g][:, :].rearrange("p (n w) -> p n w", n=2 * HP), ps.rearrange("p (n w) -> p n w", n=2 * HP),
                                          bc("g0_bkv", UNITS).rearrange("p (n w) -> p n w", n=2 * HP), ALU.add).then_inc(sig["g0_kv"], 1)

                    def subtract_high(g):
                        after(dve, "g0_hi", g)
                        dve.tensor_tensor(kv[g][:, :], kv[g][:, :], kvc[g][:, 0, :], ALU.subtract).then_inc(sig["g0_rest"], 1)

                    def low_parts(g):
                        after(dve, "g0_mid", g)
                        dve.tensor_tensor(kvc[g][:, 2, :], kv[g][:, :], kvc[g][:, 1, :], ALU.subtract).then_inc(sig["g0_lo"], 1)

                    def positions(g):
                        ps = fullM(dve, "g0_off", g)
                        dve.scalar_tensor_tensor(out=pos[g][:, :], in0=ps[:, 0:NS], scalar=W["query_pos"][:, 0:1],
                                                 in1=bc("off", NS), op0=ALU.add, op1=ALU.add).then_inc(sig["g0_pos"], 1)

                    def hat_weights(g):
                        after(dve, "g0_hat", g)
                        for e in range(2):
                            link(dve.tensor_scalar(hat[g][:, :, e, :], dist[g][:, e, :].rearrange("p (n h) -> p n h", h=2),
                                                   -1.0, 1.0, ALU.mult, ALU.add))
                        hh = hat[g][:, :, :, :].rearrange("p n e h -> p (n e h)")
                        link(dve.tensor_scalar(hh, hh, 0.0, None, ALU.max))

                    def sampled_attention(g):
                        n40 = HP * NK
                        after(dve, "g0_products", g)
                        sc = wts[g]
                        link(dve.tensor_reduce(sc[:, :], bigp[g][:, :].rearrange("p (n d) -> p n d", d=D8), AX, ALU.add))
                        hh = hat[g][:, :, :, :].rearrange("p n e h -> p (n e h)")
                        link(dve.tensor_tensor(sc[:, :], sc[:, :], hh, ALU.mult))
                        sv = sc[:, :].rearrange("p (n e h) -> p n e h", e=2, h=2)
                        s1 = small[g][:, 1, :]
                        s1n = s1.rearrange("p (n h) -> p n h", h=2)
                        link(dve.tensor_tensor(s1n, sv[:, :, 0, :], sv[:, :, 1, :], ALU.add))
                        by_head = s1.rearrange("p (n k h) -> p n h k", n=HP, h=2)
                        mx = rmax[g][:, :].rearrange("p (n h) -> p n h", h=2)
                        link(dve.tensor_reduce(mx, by_head, AX, ALU.max))
                        k3 = s1.rearrange("p (n k h) -> p n k h", n=HP, h=2)
                        mxb = spread(mx, 2, NK)
                        dve.tensor_tensor(k3, k3, mxb, ALU.subtract).then_inc(sig["g0_shifted"], 1)

                    def sampled_values(g):
                        sc, s1 = wts[g], small[g][:, 1, :]
                        s1n = s1.rearrange("p (n h) -> p n h", h=2)
                        sv = sc[:, :].rearrange("p (n e h) -> p n e h", e=2, h=2)
                        by_head = s1.rearrange("p (n k h) -> p n h k", n=HP, h=2)
                        k3 = s1.rearrange("p (n k h) -> p n k h", n=HP, h=2)
                        mx = rmax[g][:, :].rearrange("p (n h) -> p n h", h=2)
                        mxb = spread(mx, 2, NK)
                        after(dve, "g0_probs", g)
                        link(dve.tensor_reduce(mx, by_head, AX, ALU.add))
                        link(dve.tensor_scalar(rmax[g][:, :], rmax[g][:, :], 2.0, None, ALU.mult))
                        link(dve.reciprocal(rmax[g][:, :], rmax[g][:, :]))
                        link(dve.tensor_tensor(k3, k3, mxb, ALU.mult))
                        dve.tensor_tensor(sv, hat[g][:, :, :, :], spread(s1n, 2, 2), ALU.mult).then_inc(sig["g0_weights"], 1)

                    def sum_samples(g):
                        after(dve, "g0_weighted", g)
                        dve.tensor_reduce(att[g][:, 0:P].rearrange("p (n w) -> p n w", n=HP),
                                          bigp[g][:, :].rearrange("p (n k w) -> p n w k", n=HP, k=2 * NK), AX, ALU.add).then_inc(sig["g0_ctx"], 1)

                    def squares(g):
                        link(dve.tensor_tensor(hbuf[g][:, :], x_f[g][:, :], x_f[g][:, :], ALU.mult))
                        dve.tensor_reduce(rstd[g][:, 0:1], hbuf[g][:, :], AX, ALU.add).then_inc(sig["f0_sq"], 1)

                    def route(g):
                        lg = small[g][:, 2, :]
                        after(dve, "f0_rnorm", g)
                        after(dve, "f0_logits", g)
                        link(dve.tensor_scalar(rstd[g][:, 0:1], rstd[g][:, 1:2], 1e12, None, ALU.min))
                        link(dve.scalar_tensor_tensor(out=lg[:, 16:24], in0=lg[:, 0:E], scalar=rstd[g][:, 0:1], in1=lg[:, E:2 * E],
                                                      op0=ALU.mult, op1=ALU.add))
                        link(dve.max(lg[:, 24:32], lg[:, 16:24]))
                        link(dve.tensor_scalar(lg[:, 32:40], lg[:, 16:24], lg[:, 25:26], None, ALU.is_ge))
                        dve.tensor_scalar(small[g][:, 1, 0:E], lg[:, 16:24], lg[:, 24:25], None, ALU.subtract).then_inc(sig["f0_shifted"], 1)

                    def route_gates(g):
                        lg = small[g][:, 2, :]
                        after(dve, "f0_exp", g)
                        link(dve.tensor_tensor(lg[:, 40:48], small[g][:, 1, 0:E], lg[:, 32:40], ALU.mult))
                        link(dve.tensor_reduce(lg[:, 48:49], lg[:, 40:48], AX, ALU.add))
                        link(dve.reciprocal(lg[:, 49:50], lg[:, 48:49]))
                        dve.tensor_scalar(small[g][:, 0, 0:E], lg[:, 40:48], lg[:, 49:50], None, ALU.mult).then_inc(sig["f0_gates"], 1)

                    def gate_hidden(g):
                        ps = fullM(dve, "f0_gb", g)
                        after(dve, "f0_h", g)
                        dve.tensor_tensor(hT[g][:, :], hT[g][:, :], ps, ALU.mult).then_inc(sig["f0_gated"], 1)

                    def mixture(g):
                        ps = fullM(dve, "f1_gs", g)
                        lg = small[g][:, 2, :]
                        dve.tensor_tensor(lg[:, 0:E], ps[:, 0:E], bc("f1_gb", E), ALU.add).then_inc(sig["f1_scored"], 1)
                        after(dve, "f1_scored", g)
                        link(dve.tensor_scalar(lg[:, 0:E], lg[:, 0:E], 1e-4, None, ALU.max))
                        link(dve.tensor_reduce(lg[:, 8:9], lg[:, 0:E], AX, ALU.max))
                        dve.tensor_scalar(small[g][:, 1, 0:E], lg[:, 0:E], lg[:, 8:9], None, ALU.subtract).then_inc(sig["f1_shifted"], 1)

                    def mixture_gates(g):
                        lg = small[g][:, 2, :]
                        after(dve, "f1_exp", g)
                        link(dve.tensor_reduce(lg[:, 9:10], small[g][:, 1, 0:E], AX, ALU.add))
                        link(dve.reciprocal(lg[:, 10:11], lg[:, 9:10]))
                        dve.tensor_scalar(lg[:, 16:24], small[g][:, 1, 0:E], lg[:, 10:11], None, ALU.mult).then_inc(sig["f1_p"], 1)

                    def mixture_weights(g):
                        lg = small[g][:, 2, :]
                        after(dve, "f1_rank", g)
                        link(dve.tensor_reduce(lg[:, 24:32], ranks[g][:, :].rearrange("p (a b) -> p a b", a=E), AX, ALU.add))
                        link(dve.tensor_scalar(lg[:, 24:32], lg[:, 24:32], 2.0, None, ALU.is_lt))
                        link(dve.tensor_scalar(lg[:, 32:40], lg[:, 16:24], 0.1, None, ALU.max))
                        link(dve.tensor_tensor(lg[:, 32:40], lg[:, 32:40], lg[:, 24:32], ALU.mult))
                        link(dve.tensor_reduce(lg[:, 11:12], lg[:, 32:40], AX, ALU.add))
                        link(dve.reciprocal(lg[:, 12:13], lg[:, 11:12]))
                        dve.tensor_scalar(small[g][:, 0, 0:E], lg[:, 32:40], lg[:, 12:13], 0.5, ALU.mult,
                                          ALU.mult).then_inc(sig["f1_gates"], 1)

                    def mixture_out(g):
                        after(dve, "f1_gates", g)
                        ps = fullS(dve, "f1_y", g)
                        dve.tensor_tensor(probs[g][:, :].rearrange("p (e f) -> p e f", e=E), ps.rearrange("p (e f) -> p e f", e=E),
                                          spread(small[g][:, 0, 0:E], 2, D), ALU.mult).then_inc(sig["f1_mixed"], 1)
                        after(dve, "f1_mixed", g)
                        link(dve.tensor_reduce(att[g][:, 0:D], probs[g][:, :].rearrange("p (e f) -> p f e", e=E), AX, ALU.add))
                        link(dve.tensor_tensor(hbuf[g][:, :], att[g][:, 0:D], x_m[g][:, :], ALU.add))

                    def finish(g):
                        ps = fullM(dve, "f1_b", g)
                        dve.tensor_tensor(hbuf[g][:, :], ps[:, 0:D], hbuf[g][:, :], ALU.add).then_inc(sig["f1_biased"], 1)
                        after(dve, "f1_biased", g)
                        moments("f1", g)

                    def output(g):
                        if g % G == 0:
                            dve.wait_ge(out_stored, done("f1") * (16 * G) + 1)
                        norm("f1", g, x_out[g][:, :]).then_inc(sig["out_x"], 1)

                    run = {"g0_B": [sample_inputs], "g0_C": [positions], "g0_B2": [subtract_high], "g0_B3": [low_parts],
                           "g0_D": [hat_weights],
                           "g0_G": [sampled_attention], "g0_G2": [sampled_values], "g0_G3": [sum_samples], "g0_H": [lambda g: residual("g0", g)],
                           "g0_I": [lambda g: hand_over("g0", g)],
                           "f0_A": [squares], "f0_B": [route], "f0_C": [route_gates], "f0_D": [gate_hidden],
                           "f0_E": [lambda g: residual("f0", g)], "f0_F": [lambda g: hand_over("f0", g)],
                           "a0_H": [inner_norm], "a0_I": [lambda g: hand_over("a0", g)],
                           "a1_H": [lambda g: hand_over("a1", g)], "a2_H": [lambda g: hand_over("a2", g)],
                           "f1_B": [mixture], "f1_B2": [mixture_gates], "f1_C": [mixture_weights, mixture_out],
                           "f1_D": [finish], "f1_E": [output]}
                    for l in ("a0", "a1", "a2"):
                        for s, f in (("C", shift), ("E", normalise), ("G", residual)):
                            run[f"{l}_{s}"] = [lambda g, l=l, f=f: f(l, g)]
                        run[f"{l}_B"] = [lambda g, l=l: masks(l, g)]
                        run[f"{l}_V"] = [lambda g, l=l: values(l, g)]
                    for stage, g in order:
                        for f in run.get(stage, ()):
                            f(g)

                @block.gpsimd
                def _(pool):
                    steps = [0]

                    def link(ins):
                        steps[0] += 1
                        ins.then_inc(pool_step, 1)
                        pool.wait_ge(pool_step, steps[0])

                    def bias_residual(l, g):
                        after(pool, f"{l}_xT", g)
                        pool.tensor_tensor(xb[g][:, :], x_of[l][g][:, :], W[f"bc_{l}_bo"][:, :], ALU.add).then_inc(sig[f"{l}_xb"], 1)

                    def rsqrt(name, g, eps):
                        after(pool, f"{name}_var", g)
                        link(pool.tensor_scalar(rstd[g][:, 0:1], mv[g][:, 1:2], eps, None, ALU.add))
                        pool.tensor_tensor(rstd[g][:, 1:2], rstd[g][:, 0:1], mhalf[:, :], ALU.pow).then_inc(sig[f"{name}_rstd"], 1)

                    def sampling_index(g):
                        t = tile(done("g0"), g)
                        w = [pw[g][:, i, :] for i in range(4)]
                        L, Linv, Lpos = (lc[g][:, i:i + 1] for i in range(3))
                        link(pool.tensor_copy(lc[g][:, :].unsqueeze(2), lens[:, :, t]))
                        after(pool, "g0_pos", g)
                        link(pool.tensor_scalar(posi[g][:, :], pos[g][:, :], Linv, None, ALU.mult))
                        link(pool.tensor_scalar(w[0], posi[g][:, :], L, None, ALU.mult))
                        link(pool.tensor_tensor(w[1], pos[g][:, :], w[0], ALU.subtract))
                        link(pool.tensor_scalar(w[0], w[1], 0.0, Lpos, ALU.is_lt, ALU.mult))
                        link(pool.tensor_tensor(w[1], w[1], w[0], ALU.add))
                        link(pool.tensor_scalar(w[0], w[1], L, Lpos, ALU.is_ge, ALU.mult))
                        link(pool.tensor_tensor(w[1], w[1], w[0], ALU.subtract))
                        link(pool.tensor_scalar(w[2], w[1], float(S) / (S - 1), -0.5, ALU.mult, ALU.add))
                        link(pool.tensor_copy(posi[g][:, :], w[2]))
                        link(pool.tensor_copy(w[1], posi[g][:, :]))
                        link(pool.tensor_tensor(w[0], w[1], w[2], ALU.subtract))
                        link(pool.tensor_scalar(w[0], w[0], 0.0, None, ALU.is_gt))
                        link(pool.tensor_tensor(w[1], w[1], w[0], ALU.subtract))
                        link(pool.tensor_scalar(w[1], w[1], 0.0, float(S - 2), ALU.max, ALU.min))
                        i0 = idx[g][:, :, 0:40]
                        pool.tensor_scalar(i0, w[1].rearrange("p (a n) -> p a n", a=2), -32.0, None,
                                           ALU.add).then_inc(sig["g0_idx"], 1)
                        after(pool, "g0_idx", g, 1)
                        pool.tensor_tensor(idx[g][:, :, 40:80], i0, i0, ALU.mult).then_inc(sig["g0_idx"], 1)
                        link(pool.tensor_tensor(dist[g][:, 0, :], w[2], w[1], ALU.subtract))
                        pool.tensor_scalar(dist[g][:, 1, :], dist[g][:, 0, :], -1.0, None, ALU.add).then_inc(sig["g0_dist"], 1)

                    def key_products(g):
                        after(pool, "g0_sampled", g)
                        after(pool, "g0_qtok", g)
                        kin = samp[g][:, :, 0:16].rearrange("p (n k) w -> p n k w", n=HP)
                        q4 = spread(q_tok[g][:, :].rearrange("p (n w) -> p n w", n=HP), 2, 2 * NK)
                        pool.tensor_tensor(bigp[g][:, :].rearrange("p (n k w) -> p n k w", n=HP, k=2 * NK), kin, q4,
                                           ALU.mult).then_inc(sig["g0_products"], 1)

                    def weigh_values(g):
                        after(pool, "g0_weights", g)
                        vin = samp[g][:, :, 16:32].rearrange("p n (h d) -> p n h d", h=2)
                        wv = spread(wts[g][:, :].rearrange("p (n h) -> p n h", h=2), 3, D8)
                        pool.tensor_tensor(bigp[g][:, :].rearrange("p (n h d) -> p n h d", h=2, d=D8), vin, wv,
                                           ALU.mult).then_inc(sig["g0_weighted"], 1)

                    def ranks_of(g):
                        after(pool, "f1_p", g)
                        p = small[g][:, 2, 16:24]
                        other = spread(p, 1, E)
                        own = spread(p, 2, E)
                        r3 = ranks[g][:, :].rearrange("p (a b) -> p a b", a=E)
                        d3 = pw[g][:, 1, 0:64].rearrange("p (a b) -> p a b", a=E)
                        e3 = pw[g][:, 0, 0:64].rearrange("p (a b) -> p a b", a=E)
                        link(pool.tensor_tensor(d3, other, own, ALU.subtract))
                        link(pool.tensor_scalar(r3, d3, 0.0, None, ALU.is_gt))
                        link(pool.tensor_scalar(e3, d3, 0.0, None, ALU.is_equal))
                        link(pool.tensor_tensor(e3, e3, W["bc_lower"][:, :].rearrange("p (a b) -> p a b", a=E), ALU.mult))
                        pool.tensor_tensor(r3, r3, e3, ALU.add).then_inc(sig["f1_rank"], 1)

                    def norm_of_x(g):
                        after(pool, "f0_sq", g)
                        pool.tensor_tensor(rstd[g][:, 1:2], rstd[g][:, 0:1], mhalf[:, :], ALU.pow).then_inc(sig["f0_rnorm"], 1)

                    run = {"a0_B": lambda g: bias_residual("a0", g), "g0_B": lambda g: bias_residual("g0", g),
                           "a2_B": lambda g: bias_residual("a2", g), "g0_C": sampling_index, "g0_G": key_products, "g0_G2": weigh_values, "f0_A": norm_of_x, "f1_B2": ranks_of,
                           "a0_G": lambda g: rsqrt("a0i", g, 1e-12), "a0_H": lambda g: rsqrt("a0", g, EPS_LN),
                           "g0_H": lambda g: rsqrt("g0", g, EPS_LN), "f0_E": lambda g: rsqrt("f0", g, EPS_LN),
                           "a1_G": lambda g: rsqrt("a1", g, EPS_LN), "a2_G": lambda g: rsqrt("a2", g, EPS_LN),
                           "f1_D": lambda g: rsqrt("f1", g, EPS_LN)}
                    for stage, g in order:
                        if stage in run:
                            run[stage](g)
            nc.all_engine_barrier(sems_to_clear=turn_sems)

        for n in range(PHASES - 1):
            turn(n, range(n + 1))
        with nc.Fori(PHASES - 1, PAIRS) as it:
            turn(it, range(PHASES))
        for n in range(1, PHASES):
            turn(PAIRS + n - 1, range(n, PHASES))
        nc.sync.wait_ge(out_stored, 16 * G * PAIRS + 1)
        nc.sync.wait_ge(x_loaded, 16 * G * (PAIRS + 1))


def _layout(i):
    import numpy as np

    f = np.float32
    c = np.ascontiguousarray
    p = np.arange(P)
    a = {"x": i["x"], "ctx": i["ctx_1024"]}
    used = i["L0_attn_dist_emb"][S:S + WIN]
    a["rel_fwd"] = c(np.tile(used.T, (H16, 1)))
    a["rel_rev"] = c(np.tile(used[::-1].T, (H16, 1)))

    def split_heads(w, heads, d):
        return w.reshape(-1, heads // 2, 2, d).transpose(0, 2, 1, 3).reshape(w.shape[0], heads * d)

    def col(v):
        return c(v.reshape(-1, P).T)

    a["a0_wq"], a["a0_wk"] = i["L0_attn_Wq"], i["L0_attn_Wk"]
    a["a0_wv"] = c(split_heads(i["L0_attn_Wv"], H16, D8))
    a["a0_wo"] = i["L0_attn_Wo"]
    a["a0_bq"], a["a0_bk"] = col(i["L0_attn_bq"]), col(i["L0_attn_bk"])
    a["bc_a0_bv"] = c(split_heads(i["L0_attn_bv"][None], H16, D8).reshape(2, S))
    a["bc_a0_bo"] = i["L0_attn_bo"][None]
    a["bc_a0_gamma"], a["bc_a0_beta"] = i["L0_attn_ln_gamma"][None], i["L0_attn_ln_beta"][None]

    a["g0_wq"] = c(i["L0_xattn_Wq"].T)
    a["g0_bq"], a["bc_g0_bq"] = col(i["L0_xattn_bq"]), i["L0_xattn_bq"][None]
    wk = split_heads(i["L0_xattn_Wk"].T, H16, D8).reshape(D, 2, HP, 1, D8)
    wv = split_heads(i["L0_xattn_Wv"].T, H16, D8).reshape(D, 2, HP, 1, D8)
    a["g0_wkv"] = c(np.concatenate([wk, wv], 3).reshape(D, 2 * P))
    bk = split_heads(i["L0_xattn_bk"][None], H16, D8).reshape(2, 1, HP, 1, 1, D8)
    bv = split_heads(i["L0_xattn_bv"][None], H16, D8).reshape(2, 1, HP, 1, 1, D8)
    a["bc_g0_bkv"] = c(np.broadcast_to(np.concatenate([bk, bv], 4), (2, 2, HP, 2, 2, D8)).reshape(2, UNITS))
    order = np.arange(H16 * NK).reshape(HP, 2, NK).transpose(0, 2, 1).reshape(-1)
    a["g0_woff"] = c(i["L0_xattn_Woff"][order].T)
    a["bc_off"] = c(i["L0_xattn_boff"][order][None])
    a["bc_ref"] = c(np.broadcast_to((np.arange(NK) - 3).astype(f)[None, :, None], (HP, NK, 2)).reshape(1, NS))
    a["g0_wo"] = c(i["L0_xattn_Wo"].T)
    a["bc_g0_bo"] = i["L0_xattn_bo"][None]
    a["mask_bs"] = i["mask_BxS2_if0"]
    a["query_pos"] = (p % S).astype(f)[:, None]
    a["seq_of_tile"] = c((p[:, None, None] == 2 * np.arange(TILES)[None, None] + np.arange(2)[None, :, None])
                         .reshape(P, 2 * TILES).astype(f))
    a["ones64"] = np.ones((P, S), f)
    spread_rows = np.zeros((81, 4, NK, 2, S), np.float16)
    j = np.arange(S) - 32
    for n in range(4):
        for k in range(NK):
            for h in range(2):
                r = (n * NK + k) * 2 + h
                spread_rows[r, n, k, h] = 2 * j
                spread_rows[40 + r, n, k, h] = -1
    spread_rows[80] = 1 - j * j
    a["spread"] = spread_rows.reshape(81, 20 * P)

    a["centroids"] = i["L0_ffn_centroids"]
    a["w_routeT"] = c(i["L0_ffn_w_route"].T)
    a["f0_w1"] = c(i["L0_ffn_w1"].transpose(1, 0, 2).reshape(D, 512))
    a["f0_b1"] = c(i["L0_ffn_b1"].reshape(4, P).T)
    a["f0_w2"] = c(i["L0_ffn_w2"].reshape(4, P, D).transpose(1, 0, 2).reshape(P, 512))
    a["f0_b2"] = i["L0_ffn_b2"]
    a["expert_rows"] = c((np.arange(E)[:, None, None] == 2 * np.arange(4)[None, :, None] + (p // 64)[None, None])
                         .reshape(E, 4 * P).astype(f))

    def split_wide(w):
        return w.reshape(w.shape[0], H8 // 2, 2, D32).transpose(0, 2, 1, 3).reshape(w.shape[0], H8 * D32)

    a["a1_wq"] = c(i["L1_attn_Wq"].T)
    a["a1_wkv"] = c(i["L1_attn_Wkv_down"].T)
    a["a1_wk"] = c(i["L1_attn_Wk_up"].T)
    a["a1_wv"] = c(split_wide(i["L1_attn_Wv_up"].T))
    a["a1_wo"] = c(i["L1_attn_Wo"].T.reshape(2, P, D).transpose(1, 0, 2).reshape(P, 2 * D))

    a["a2_wq"], a["a2_wk"] = c(i["L1_xattn_Wq"].T), c(i["L1_xattn_Wk"].T)
    a["a2_wv"] = c(split_heads(i["L1_xattn_Wv"].T, H16, D8))
    a["a2_wo"] = c(i["L1_xattn_Wo"].T)
    a["a2_bq"], a["a2_bk"] = col(i["L1_xattn_bq"]), col(i["L1_xattn_bk"])
    a["bc_a2_bv"] = c(split_heads(i["L1_xattn_bv"][None], H16, D8).reshape(2, S))
    a["bc_a2_bo"] = i["L1_xattn_bo"][None]
    a["mask_ss"] = c(i["mask_1x1xSxS2_if1"].reshape(S, S))

    a["f1_gw"] = i["L1_ffn_gate_W"]
    a["bc_f1_gb"] = i["L1_ffn_gate_b"][None]
    a["f1_w"] = c(i["L1_ffn_expert_W"].transpose(1, 0, 2).reshape(D, E * D))
    a["f1_b"] = i["L1_ffn_expert_b"]
    e = np.arange(E)
    a["bc_lower"] = (e[None, :] < e[:, None]).reshape(1, E * E).astype(f)

    a["ident"] = np.eye(P, dtype=f)
    a["head16"] = (p[:, None] // D8 == np.arange(H16)[None]).astype(f)
    a["within4"] = (p[:, None] // D8 % 4 == np.arange(4)[None]).astype(f)
    a["group4"] = (p[:, None] // 32 == np.arange(4)[None]).astype(f)
    return {k: c(v) for k, v in a.items()}


def kernel(**inputs):
    import numpy as _np
    import concourse.bacc as _bacc
    from concourse import mybir as _mybir
    from concourse.bass_utils import run_bass_kernel_spmd as _run

    nc = _bacc.Bacc("TRN2", target_bir_lowering=False, num_devices=1)
    arrays, args = {}, {}
    for name, a in _layout({k: _np.asarray(v) for k, v in inputs.items()}).items():
        arrays[f"in_{name}"] = a
        args[name] = nc.dram_tensor(f"in_{name}", a.shape, _mybir.dt.from_np(a.dtype), kind="ExternalInput").ap()
    out = nc.dram_tensor("out_0", (B, S, D), _mybir.dt.float32, kind="ExternalOutput").ap()
    decoder_kernel(nc, args, out)
    r = _run(nc, [arrays], core_ids=[0])
    return r.results[0]["out_0"]
```
